# Optimizing a Trainium2 kernel written in Bass

```python
import numpy as np
import jax
import jax.numpy as jnp

def _softmax(x, axis=-1):
    return jax.nn.softmax(x, axis=axis)

def _gelu(x):
    return jax.nn.gelu(x, approximate=True)

def _silu(x):
    return jax.nn.silu(x)

def _sigmoid(x):
    return jax.nn.sigmoid(x)

def _layernorm(x, axis=-1, eps=1e-05):
    m = jnp.mean(x, axis=axis, keepdims=True)
    v = jnp.var(x, axis=axis, keepdims=True)
    return (x - m) / jnp.sqrt(v + eps)

def _scatter_add(tgt, idx, src, axis=0):
    return tgt.at[idx].add(src)

def _segment_sum(src, seg, n):
    return jax.ops.segment_sum(src, seg, n)
kernel_name = 'mk_macaron_d1_jaxref_r8_06abbe'

def setup_inputs(seed: int=0):
    np.random.seed(seed)
    _w = jnp.asarray

    def _L0_attn_setup():
        import jax, jax.numpy as jnp
        import numpy as np
        EMBED = 128
        HEADS = 16
        key = jax.random.key(seed)
        ks = jax.random.split(key, 6)
        N, S = (1, 512)
        half = EMBED // 2
        x = jax.random.normal(ks[0], (N, S, EMBED), dtype=jnp.float32)
        Wq = jax.random.normal(ks[1], (half, half), dtype=jnp.float32) * 0.02
        Wk = jax.random.normal(ks[2], (half, half), dtype=jnp.float32) * 0.02
        Wv = jax.random.normal(ks[3], (half, half), dtype=jnp.float32) * 0.02
        Wo = jax.random.normal(ks[4], (EMBED, half), dtype=jnp.float32) * 0.02
        bo = jnp.zeros((EMBED,), dtype=jnp.float32)
        return {'x': x, 'Wq': Wq, 'Wk': Wk, 'Wv': Wv, 'Wo': Wo, 'bo': bo}
    _L0_attn_in = _L0_attn_setup()

    def _L0_ffn_setup():
        import jax, jax.numpy as jnp
        import numpy as np
        E, TOP_K, D, H = (8, 2, 128, 256)
        B, S = (2, 256)
        key = jax.random.key(seed)
        ks = jax.random.split(key, 10)
        s = 0.02
        return {'x': jax.random.normal(ks[0], (B, S, D), dtype=jnp.float32), 'gate_w': jax.random.normal(ks[1], (E, D), dtype=jnp.float32) * s, 'gate_b': jnp.zeros((E,), dtype=jnp.float32), 'w0': jax.random.normal(ks[2], (E, H, D), dtype=jnp.float32) * s, 'b0': jnp.zeros((E, H), dtype=jnp.float32), 'w1': jax.random.normal(ks[3], (E, H, D), dtype=jnp.float32) * s, 'b1': jnp.zeros((E, H), dtype=jnp.float32), 'w2': jax.random.normal(ks[4], (E, D, H), dtype=jnp.float32) * s, 'b2': jnp.zeros((E, D), dtype=jnp.float32)}
    _L0_ffn_in = _L0_ffn_setup()
    _d = {'L0_attn_x': _L0_attn_in['x'], 'L0_attn_Wq': _L0_attn_in['Wq'], 'L0_attn_Wk': _L0_attn_in['Wk'], 'L0_attn_Wv': _L0_attn_in['Wv'], 'L0_attn_Wo': _L0_attn_in['Wo'], 'L0_attn_bo': _L0_attn_in['bo'], 'L0_ffn_gate_w': _L0_ffn_in['gate_w'], 'L0_ffn_gate_b': _L0_ffn_in['gate_b'], 'L0_ffn_w0': _L0_ffn_in['w0'], 'L0_ffn_b0': _L0_ffn_in['b0'], 'L0_ffn_w1': _L0_ffn_in['w1'], 'L0_ffn_b1': _L0_ffn_in['b1'], 'L0_ffn_w2': _L0_ffn_in['w2'], 'L0_ffn_b2': _L0_ffn_in['b2']}
    _x0 = _d['L0_attn_x']
    _d['L0_attn_x'] = jax.random.normal(jax.random.fold_in(jax.random.key(seed), 1), (16, 256, 128), dtype=_x0.dtype)
    del _x0
    return _d

def reference(L0_attn_x, L0_attn_Wq, L0_attn_Wk, L0_attn_Wv, L0_attn_Wo, L0_attn_bo, L0_ffn_gate_w, L0_ffn_gate_b, L0_ffn_w0, L0_ffn_b0, L0_ffn_w1, L0_ffn_b1, L0_ffn_w2, L0_ffn_b2):

    def _L0_attn_ref(x, Wq, Wk, Wv, Wo, bo):
        import jax, jax.numpy as jnp
        import numpy as np
        EMBED = 128
        HEADS = 16
        N, S, E = x.shape
        H = HEADS
        Dh = E // 2 // H
        scale = float(E // H) ** 0.5
        left = x[..., :E // 2]
        q = (left @ Wq.T).reshape(N, S, H, Dh)
        k = (left @ Wk.T).reshape(N, S, H, Dh)
        v = (left @ Wv.T).reshape(N, S, H, Dh)
        energy = jnp.einsum('nqhd,nkhd->nqkh', q, k)
        att = jax.nn.softmax(energy / scale, axis=2)
        out = jnp.einsum('nqkh,nkhd->nqhd', att, v)
        out = out.reshape(N, S, E // 2)
        return out @ Wo.T + bo

    def _L0_ffn_ref(x, gate_w, gate_b, w0, b0, w1, b1, w2, b2):
        import jax, jax.numpy as jnp
        import numpy as np
        E, TOP_K, D, H = (8, 2, 128, 256)
        B, S = (2, 256)
        Bn, Sq, Dv = x.shape
        xt = x.reshape(-1, Dv)
        logits = xt @ gate_w.T + gate_b
        top_v, top_i = jax.lax.top_k(logits, TOP_K)
        h0 = jnp.einsum('td,ehd->eth', xt, w0) + b0[:, None, :]
        h1 = jnp.einsum('td,ehd->eth', xt, w1) + b1[:, None, :]
        act = h0 * jax.nn.silu(h1)
        out_all = jnp.einsum('eth,edh->etd', act, w2) + b2[:, None, :]
        out_te = jnp.transpose(out_all, (1, 0, 2))
        sel = jnp.take_along_axis(out_te, top_i[:, :, None], axis=1)
        w = jax.nn.softmax(top_v, axis=-1)[:, :, None]
        out = (w * sel).sum(axis=1)
        return out.reshape(Bn, Sq, Dv)
    x = L0_attn_x
    x = x + 0.5 * _L0_ffn_ref(_layernorm(x, axis=-1), L0_ffn_gate_w, L0_ffn_gate_b, L0_ffn_w0, L0_ffn_b0, L0_ffn_w1, L0_ffn_b1, L0_ffn_w2, L0_ffn_b2)
    x = x + _L0_attn_ref(_layernorm(x, axis=-1), L0_attn_Wq, L0_attn_Wk, L0_attn_Wv, L0_attn_Wo, L0_attn_bo)
    x = x + 0.5 * _L0_ffn_ref(_layernorm(x, axis=-1), L0_ffn_gate_w, L0_ffn_gate_b, L0_ffn_w0, L0_ffn_b0, L0_ffn_w1, L0_ffn_b1, L0_ffn_w2, L0_ffn_b2)
    return x

_drawn_inputs = setup_inputs


def setup_inputs(seed=0):
    import zlib

    import numpy as np

    out = dict(_drawn_inputs(seed))
    spreads = {'L0_attn_bo': (0.0, 0.1),
     'L0_ffn_gate_b': (0.0, 0.1),
     'L0_ffn_b0': (0.0, 0.8),
     'L0_ffn_b1': (0.0, 0.8),
     'L0_ffn_b2': (0.0, 0.1)}
    factors = {'L0_attn_Wq': 8.0,
     'L0_attn_Wk': 8.0,
     'L0_attn_Wv': 8.0,
     'L0_attn_Wo': 8.0,
     'L0_ffn_w0': 8.0,
     'L0_ffn_w1': 8.0,
     'L0_ffn_w2': 7.903}
    for name, (base, spread) in spreads.items():
        noise = np.random.default_rng([zlib.crc32(name.encode()), seed]).standard_normal(out[name].shape)
        drawn = base * np.exp(spread * noise) if base else spread * noise
        out[name] = jnp.asarray(drawn.astype(out[name].dtype))
    for name, factor in factors.items():
        out[name] = (out[name] * factor).astype(out[name].dtype)
    return out
```

```python
from contextlib import ExitStack

import concourse.bass as bass
from concourse import mybir

ALU = mybir.AluOpType
ACT = mybir.ActivationFunctionType
AX = mybir.AxisListType
F32 = mybir.dt.float32
F32R = mybir.dt.float32r
BF16 = mybir.dt.bfloat16
U32 = mybir.dt.uint32

P = 128
NB, S = 16, 256
TILES = NB * S // P
E, HID = 8, 256
CH = HID // P
T = 512
TG = T // P
GROUPS = NB * S // T
UNITS = E * CH
NH, DH, HALF = 16, 4, 64
EPS = 1e-5
FIRST = 2
LAG = 3
HEAD = LAG + 1


def wait(eng, sem, value):
    if isinstance(value, int) and value <= 0:
        return
    eng.wait_ge(sem, value)


def macaron(nc, x, gate_wT, gate_b, w0T, b0T, w1T, b1T, w2T, b2, wqT, wkT, wvT, woT, bo, out):
    x_dram = x.rearrange("b (p j) d -> p b j d", j=2)
    out_dram = out.rearrange("b (p j) d -> p b j d", j=2)
    qk_dram = nc.dram_tensor("qk_pieces", [NB, 2, 3, HALF, S], BF16)
    gate_dram = nc.dram_tensor("gates", [2, GROUPS, E, T], F32)

    with ExitStack() as ctx:
        def sb(name, shape, dt=F32, c=ctx):
            return c.enter_context(nc.sbuf_tensor(name, shape, dt))

        xs = sb("x_tokens", [P, TILES, P])
        ident = sb("ident", [P, P])
        identb = sb("identb", [P, P], BF16)
        w_hi = [sb(f"w{i}_hi", [P, E * HID], F32R) for i in range(3)]
        w_lo = [sb(f"w{i}_lo", [P, E * HID], F32R) for i in range(3)]
        b2_hi, b2_lo = sb("b2_hi", [P, P], F32R), sb("b2_lo", [P, P], F32R)
        wqk_hi, wqk_lo = sb("wqk_hi", [P, P], F32R), sb("wqk_lo", [P, P], F32R)
        wv_hi, wv_lo = sb("wv_hi", [P, HALF], F32R), sb("wv_lo", [P, HALF], F32R)
        wo_hi, wo_lo = sb("wo_hi", [P, P], F32R), sb("wo_lo", [P, P], F32R)
        gw = sb("gate_w_sb", [P, E])
        gb = sb("gate_b_sb", [P, E])
        bias0 = sb("bias0", [P, UNITS])
        bias1 = sb("bias1", [P, UNITS])
        bo_sb = sb("bo_sb", [P, P])
        iota = sb("iota", [P, E])
        neg_half = sb("neg_half", [P, TG])
        eps_sb = sb("eps_sb", [P, TG])
        ps = ctx.enter_context(nc.psum_tensor("ps", [P, 8, T], F32))

        setup(nc, dict(w0T=w0T, w1T=w1T, w2T=w2T, b2=b2, wqT=wqT, wkT=wkT, wvT=wvT, woT=woT, bo=bo,
                       gate_wT=gate_wT, gate_b=gate_b, b0T=b0T, b1T=b1T, x=x_dram),
              xs, ident, identb, w_hi, w_lo, b2_hi, b2_lo, wqk_hi, wqk_lo, wv_hi, wv_lo, wo_hi,
              wo_lo, gw, gb, bias0, bias1, bo_sb, iota, neg_half, eps_sb)
        weights = (w_hi, w_lo, b2_hi, b2_lo, gw, gb, bias0, bias1, iota, neg_half, eps_sb)
        ffn(nc, "ffn1", xs, ident, weights, gate_dram[0], ps, None)
        attention(nc, xs, ident, identb, wqk_hi, wqk_lo, wv_hi, wv_lo, wo_hi, wo_lo, bo_sb,
                  eps_sb, neg_half, qk_dram, ps)
        ffn(nc, "ffn2", xs, ident, weights, gate_dram[1], ps, out_dram)


def setup(nc, dram, xs, ident, identb, w_hi, w_lo, b2_hi, b2_lo, wqk_hi, wqk_lo, wv_hi, wv_lo,
          wo_hi, wo_lo, gw, gb, bias0, bias1, bo_sb, iota, neg_half, eps_sb):
    with ExitStack() as c:
        def sb(name, shape, dt=F32):
            return c.enter_context(nc.sbuf_tensor(name, shape, dt))

        stage = [sb(f"stage{i}", [P, E * HID]) for i in range(3)]
        b2_f, wqk_f = sb("b2_f", [P, P]), sb("wqk_f", [P, P])
        wv_f, wo_f = sb("wv_f", [P, HALF]), sb("wo_f", [P, P])
        iota_i = sb("iota_i", [P, E], mybir.dt.int32)
        w_loaded = [c.enter_context(nc.semaphore(f"w{i}_loaded")) for i in range(3)]
        small_loaded = c.enter_context(nc.semaphore("small_loaded"))
        other_loaded = c.enter_context(nc.semaphore("other_loaded"))
        x_loaded = c.enter_context(nc.semaphore("x_loaded"))
        b2_zero = c.enter_context(nc.semaphore("b2_zero"))
        ident_step = c.enter_context(nc.semaphore("ident_step"))
        hi_done = c.enter_context(nc.semaphore("hi_done"))
        block = c.enter_context(nc.Block())
        pairs = [(b2_f, b2_hi, b2_lo), (wqk_f, wqk_hi, wqk_lo), (wv_f, wv_hi, wv_lo),
                 (wo_f, wo_hi, wo_lo)] + [(stage[i], w_hi[i], w_lo[i]) for i in range(3)]

        @block.sync
        def _(sp):
            sp.wait_ge(b2_zero, 1)
            for dst, name in ((b2_f[0:E, :], "b2"), (wqk_f[0:HALF, 0:HALF], "wqT"),
                              (wqk_f[HALF:P, 0:HALF], "wqT"), (wqk_f[0:HALF, HALF:P], "wkT"),
                              (wqk_f[HALF:P, HALF:P], "wkT"), (wv_f[0:HALF, :], "wvT"),
                              (wv_f[HALF:P, :], "wvT"), (wo_f[0:HALF, :], "woT"),
                              (wo_f[HALF:P, :], "woT")):
                sp.dma_start(dst, dram[name]).then_inc(small_loaded, 16)
            for i, name in enumerate(("w0T", "w1T", "w2T")):
                sp.dma_start(stage[i][:], dram[name]).then_inc(w_loaded[i], 16)
            sp.wait_ge(small_loaded, 9 * 16)

        @block.scalar
        def _(act):
            for dst, name in ((gw[:], "gate_wT"), (bias0[:], "b0T"), (bias1[:], "b1T")):
                act.dma_start(dst, dram[name]).then_inc(other_loaded, 16)
            act.dma_start(gb[:], dram["gate_b"].partition_broadcast(P)).then_inc(other_loaded, 16)
            act.dma_start(bo_sb[:], dram["bo"].partition_broadcast(P)).then_inc(other_loaded, 16)
            xv = xs.rearrange("p (b j) d -> p b j d", j=2)
            for b in range(0, NB, 2):
                act.dma_start(xv[:, b:b + 2], dram["x"][:, b:b + 2]).then_inc(x_loaded, 16)
            for k, (full, hi, _) in enumerate(pairs):
                if k == 0:
                    act.wait_ge(small_loaded, 9 * 16)
                if k >= 4:
                    act.wait_ge(w_loaded[k - 4], 16)
                nc.scalar.activation(hi[:], full[:], ACT.Copy).then_inc(hi_done, 1)
            act.wait_ge(other_loaded, 5 * 16)
            act.wait_ge(x_loaded, (NB // 2) * 16)

        @block.gpsimd
        def _(pool):
            nc.gpsimd.memset(b2_f[:], 0.0).then_inc(b2_zero, 1)
            nc.gpsimd.memset(ident[:], 0.0).then_inc(ident_step, 1)
            nc.gpsimd.iota(iota_i[:], pattern=[[1, E]], base=0, channel_multiplier=0).then_inc(ident_step, 1)
            pool.wait_ge(ident_step, 2)
            nc.gpsimd.affine_select(out=ident[:], in_=ident[:], compare_op=ALU.not_equal, fill=1.0,
                                    base=0, pattern=[[-1, P]], channel_multiplier=1).then_inc(ident_step, 1)

        @block.vector
        def _(dve):
            dve.wait_ge(ident_step, 3)
            nc.vector.tensor_copy(identb[:], ident[:])
            nc.vector.tensor_copy(iota[:], iota_i[:])
            nc.vector.memset(neg_half[:], -0.5)
            nc.vector.memset(eps_sb[:], EPS)
            for k, (full, hi, lo) in enumerate(pairs):
                dve.wait_ge(hi_done, k + 1)
                nc.vector.tensor_tensor(lo[:], full[:], hi[:].bitcast(F32), ALU.subtract)


def ffn(nc, name, xs, ident, weights, gate_dram, ps, out_dram):
    w_hi, w_lo, b2_hi, b2_lo, gw, gb, bias0, bias1, iota, neg_half, eps_sb = weights
    H1, H0, Y, XT, LG, GT = (0, 1), (2, 3), 4, 5, 6, 7
    with ExitStack() as c:
        def sb(n, shape, dt=F32):
            return c.enter_context(nc.sbuf_tensor(f"{name}_{n}", shape, dt))

        def sem(n):
            return c.enter_context(nc.semaphore(f"{name}_{n}"))

        gates_bc = sb("gates_bc", [P, 2, E, T])
        stats, mv = sb("stats", [P, TG, 6]), sb("mv", [P, TG, 2])
        vare, rstd = sb("vare", [P, TG]), sb("rstd", [P, TG])
        xn = sb("xn", [P, TG, P])
        xf = sb("xf", [P, T])
        x_hi, x_lo = sb("x_hi", [P, 2, T], F32R), sb("x_lo", [P, 2, T], F32R)
        logits, top = sb("logits", [P, TG, E]), sb("top", [P, TG, E])
        top_i, top_f = sb("top_i", [P, TG, E], U32), sb("top_f", [P, TG, 2])
        diff, th, w12 = sb("diff", [P, TG]), sb("th", [P, TG]), sb("w12", [P, 2, TG])
        pick = sb("pick", [P, 2, TG, E])
        gpad = sb("gpad", [P, TG, P])
        g_hi, g_lo, g_f = sb("g_hi", [P, T], F32R), sb("g_lo", [P, T], F32R), sb("g_f", [E, T])
        silu = sb("silu", [P, 2, T])
        gated = sb("gated", [P, 2, T])
        act_sb = sb("act", [P, 4, T])
        act_hi, act_lo = sb("act_hi", [P, 4, T], F32R), sb("act_lo", [P, 4, T], F32R)
        y_sb = sb("y_sb", [P, T])
        spare = sb("spare", [P, 2])

        stats_ready, rstd_step, xn_ready = sem("stats_ready"), sem("rstd_step"), sem("xn_ready")
        xT_ready, xf_ready, xsplit_ready = sem("xT_ready"), sem("xf_ready"), sem("xsplit_ready")
        logits_ready, diff_ready, tanh_ready = sem("logits_ready"), sem("diff_ready"), sem("tanh_ready")
        gates_ready, gT_ready, gf_ready = sem("gates_ready"), sem("gT_ready"), sem("gf_ready")
        gsplit_ready, gates_out, gates_in = sem("gsplit_ready"), sem("gates_out"), (sem("gates_in_first"), sem("gates_in_rest"))
        h1_ready, h0_ready, silu_done = sem("h1_ready"), sem("h0_ready"), sem("silu_done")
        gated_done, act_done, hi_done, lo_done = sem("gated_done"), sem("act_done"), sem("hi_done"), sem("lo_done")
        w2_done = sem("w2_done")
        y_ready, y_copied, yT_ready = sem("y_ready"), sem("y_copied"), sem("yT_ready")
        x_updated, stored = sem("x_updated"), sem("stored")
        bn_done, xhi_done, logits_done, top_done = sem("bn_done"), sem("xhi_done"), sem("logits_done"), sem("top_done")
        index_done, topf_done, w12_done = sem("index_done"), sem("topf_done"), sem("w12_done")
        match_done, pick_done, ghi_done, gpad_zero = sem("match_done"), sem("pick_done"), sem("ghi_done"), sem("gpad_zero")
        block = c.enter_context(nc.Block())

        def pe_first(pe, g, u, par):
            e, k = divmod(u, CH)
            cols = slice(e * HID + k * P, e * HID + k * P + P)
            U = g * UNITS + u
            if u == 0:
                wait(pe, xsplit_ready, g + 1)
            for bank, w, ready, free in ((H1[u % 2], 1, h1_ready, silu_done),
                                         (H0[u % 2], 0, h0_ready, act_done)):
                if not (isinstance(U, int) and U < 2):
                    wait(pe, free, U - 1)
                o = ps[:, bank, :]
                pe.matmul(o, w_hi[w][:, cols], x_hi[:, par, :], start=True, stop=False)
                pe.matmul(o, w_hi[w][:, cols], x_lo[:, par, :], start=False, stop=False)
                pe.matmul(o, w_lo[w][:, cols], x_hi[:, par, :], start=False, stop=True).then_inc(ready, 1)

        def pe_second(pe, g, u):
            U = g * UNITS + u
            o = ps[:, Y, :]
            if u == 0:
                wait(pe, gsplit_ready, g + 1)
                if not (isinstance(g, int) and g == 0):
                    wait(pe, y_copied, g)
                pe.matmul(o, b2_hi[:], g_hi[:], start=True, stop=False)
                pe.matmul(o, b2_hi[:], g_lo[:], start=False, stop=False)
                pe.matmul(o, b2_lo[:], g_hi[:], start=False, stop=False)
            ws = slice(u * P, u * P + P)
            wait(pe, hi_done, U + 1)
            pe.matmul(o, w_hi[2][:, ws], act_hi[:, u % 4, :], start=False, stop=False)
            pe.matmul(o, w_lo[2][:, ws], act_hi[:, u % 4, :], start=False, stop=False)
            wait(pe, lo_done, U + 1)
            mm = pe.matmul(o, w_hi[2][:, ws], act_lo[:, u % 4, :], start=False, stop=(u == UNITS - 1))
            mm.then_inc(w2_done, 1)

        def pe_norm(pe, g):
            wait(pe, xn_ready, g + 1)
            if not (isinstance(g, int) and g < 2):
                wait(pe, x_updated, g - 1)
            for t in range(TG):
                mm = pe.transpose(ps[:, XT, t * P:(t + 1) * P], xn[:, t, :], ident[:])
            mm.then_inc(xT_ready, 1)

        def pe_logits(pe, g):
            wait(pe, xf_ready, g + 1)
            for t in range(TG):
                mm = pe.matmul(ps[:, LG, t * E:(t + 1) * E], xf[:, t * P:(t + 1) * P], gw[:], start=True, stop=True)
            mm.then_inc(logits_ready, 1)

        def pe_gates(pe, g):
            wait(pe, gates_ready, g + 1)
            for t in range(TG):
                mm = pe.transpose(ps[:, GT, t * P:(t + 1) * P], gpad[:, t, :], ident[:])
            mm.then_inc(gT_ready, 1)

        def pe_close(pe, g):
            wait(pe, y_copied, g + 1)
            wait(pe, xsplit_ready, (g + 2) if not (isinstance(g, int) and g == GROUPS - 1) else g + 1)
            for t in range(TG):
                mm = pe.transpose(ps[:, XT, t * P:(t + 1) * P], y_sb[:, t * P:(t + 1) * P], ident[:])
            mm.then_inc(yT_ready, 1)

        def pe_group(pe, g, last):
            par, nxt = g % 2, (g + 1) % 2
            for v in range(HEAD, UNITS + HEAD):
                if v < UNITS:
                    pe_first(pe, g, v, par)
                elif not last:
                    pe_first(pe, g + 1, v - UNITS, nxt)
                if v - LAG < UNITS:
                    pe_second(pe, g, v - LAG)
                if not last:
                    if v == 4:
                        pe_norm(pe, g + 1)
                    if v == 6:
                        pe_logits(pe, g + 1)
                    if v == 11:
                        pe_gates(pe, g + 1)
            pe_close(pe, g)
            if not last:
                pe_second(pe, g + 1, 0)

        @block.tensor
        def _(pe):
            pe_norm(pe, 0)
            pe_logits(pe, 0)
            pe_gates(pe, 0)
            for u in range(HEAD):
                pe_first(pe, 0, u, 0)
            pe_second(pe, 0, 0)
            with pe.Fori(0, GROUPS - 1) as g:
                pe_group(pe, g, False)
            pe_group(pe, GROUPS - 1, True)

        def act_unit(act, g, u):
            U = g * UNITS + u
            wait(act, h1_ready, U + 1)
            if not (isinstance(U, int) and U < 2):
                wait(act, gated_done, U - 1)
            nc.scalar.activation(silu[:, u % 2, :], ps[:, H1[u % 2], :], ACT.Silu,
                                 bias=bias1[:, u:u + 1]).then_inc(silu_done, 1)

        def act_hi_part(act, g, u):
            U = g * UNITS + u
            wait(act, act_done, U + 1)
            if not (isinstance(U, int) and U < 4):
                wait(act, w2_done, U - 3)
            nc.scalar.activation(act_hi[:, u % 4, :], act_sb[:, u % 4, :], ACT.Copy).then_inc(hi_done, 1)

        def act_xf(act, g):
            wait(act, xT_ready, g + 1)
            if not (isinstance(g, int) and g == 0):
                wait(act, logits_ready, g)
            nc.scalar.activation(xf[:], ps[:, XT, :], ACT.Copy).then_inc(xf_ready, 1)

        def act_tanh(act, g):
            wait(act, diff_ready, g + 1)
            nc.scalar.activation(th[:], diff[:], ACT.Tanh, scale=0.5).then_inc(tanh_ready, 1)

        def act_gf(act, g):
            wait(act, gT_ready, g + 1)
            if not (isinstance(g, int) and g == 0):
                wait(act, gates_out, g * 16)
            nc.scalar.activation(g_f[:], ps[0:E, GT, :], ACT.Copy).then_inc(gf_ready, 1)

        def act_y(act, g):
            wait(act, w2_done, (g + 1) * UNITS)
            if not (isinstance(g, int) and g == 0):
                wait(act, yT_ready, g)
            nc.scalar.activation(y_sb[:], ps[:, Y, :], ACT.Copy).then_inc(y_copied, 1)

        def act_group(act, g, last):
            for v in range(HEAD, UNITS + HEAD):
                if v == UNITS + LAG:
                    act_y(act, g)
                if v < UNITS:
                    act_unit(act, g, v)
                elif not last:
                    act_unit(act, g + 1, v - UNITS)
                if v - 1 < UNITS:
                    act_hi_part(act, g, v - 1)
                elif not last:
                    act_hi_part(act, g + 1, v - 1 - UNITS)
                if not last:
                    if v == 5:
                        act_xf(act, g + 1)
                    if v == 9:
                        act_tanh(act, g + 1)
                    if v == 12:
                        act_gf(act, g + 1)

        @block.scalar
        def _(act):
            act_xf(act, 0)
            act_tanh(act, 0)
            act_gf(act, 0)
            for u in range(HEAD):
                act_unit(act, 0, u)
                if u:
                    act_hi_part(act, 0, u - 1)
            with act.Fori(0, GROUPS - 1) as g:
                act_group(act, g, False)
            act_group(act, GROUPS - 1, True)

        def pool_unit(pool, g, u, par):
            U = g * UNITS + u
            if not (isinstance(U, int) and U < 2):
                wait(pool, act_done, U - 1)
            if u in (0, FIRST * CH):
                wait(pool, gates_in[u > 0], (g + 1) * 16)
            wait(pool, silu_done, U + 1)
            nc.gpsimd.tensor_tensor(gated[:, u % 2, :], silu[:, u % 2, :], gates_bc[:, par, u // CH, :],
                                    ALU.mult).then_inc(gated_done, 1)

        def pool_rstd(pool, g):
            wait(pool, stats_ready, g + 1)
            nc.gpsimd.tensor_tensor(vare[:], mv[:, :, 1], eps_sb[:], ALU.add).then_inc(rstd_step, 1)
            pool.wait_ge(rstd_step, 2 * g + 1)
            nc.gpsimd.tensor_tensor(rstd[:], vare[:], neg_half[:], ALU.pow).then_inc(rstd_step, 1)

        def pool_group(pool, g, par, last):
            for v in range(HEAD, UNITS + HEAD):
                if v < UNITS:
                    pool_unit(pool, g, v, par)
                elif not last:
                    pool_unit(pool, g + 1, v - UNITS, 1 - par)
                if v == 15 and not last:
                    pool_rstd(pool, g + 2)

        @block.gpsimd
        def _(pool):
            pool_rstd(pool, 0)
            pool_rstd(pool, 1)
            for u in range(HEAD):
                pool_unit(pool, 0, u, 0)
            with pool.Fori(0, GROUPS // 2 - 1) as turn:
                pool_group(pool, 2 * turn, 0, False)
                pool_group(pool, 2 * turn + 1, 1, False)
            pool_group(pool, GROUPS - 2, 0, False)
            pool_group(pool, GROUPS - 1, 1, True)

        def dve_unit(dve, g, u):
            U = g * UNITS + u
            wait(dve, h0_ready, U + 1)
            wait(dve, gated_done, U + 1)
            if not (isinstance(U, int) and U < 4):
                wait(dve, hi_done, U - 3)
                wait(dve, lo_done, U - 3)
            nc.vector.scalar_tensor_tensor(out=act_sb[:, u % 4, :], in0=ps[:, H0[u % 2], :],
                                           scalar=bias0[:, u:u + 1], in1=gated[:, u % 2, :],
                                           op0=ALU.add, op1=ALU.mult).then_inc(act_done, 1)

        def dve_lo_part(dve, g, u):
            U = g * UNITS + u
            wait(dve, hi_done, U + 1)
            if not (isinstance(U, int) and U < 4):
                wait(dve, w2_done, U - 3)
            nc.vector.tensor_tensor(act_lo[:, u % 4, :], act_sb[:, u % 4, :],
                                    act_hi[:, u % 4, :].bitcast(F32), ALU.subtract).then_inc(lo_done, 1)

        def dve_stats(dve, g):
            gx = g % GROUPS
            if not (isinstance(g, int) and g == 0):
                wait(dve, xn_ready, g)
            for t in range(TG):
                i = nc.vector.bn_stats(stats[:, t, :], xs[:, gx * TG + t, :])
            i.then_inc(bn_done, 1)
            dve.wait_ge(bn_done, g + 1)
            nc.vector.memset(spare[:, 0:1], 0.0)
            for t in range(TG):
                i = nc.vector.bn_aggr(mv[:, t, :], stats[:, t, :])
            i.then_inc(stats_ready, 1)

        def dve_norm(dve, g):
            wait(dve, rstd_step, 2 * g + 2)
            if not (isinstance(g, int) and g == 0):
                wait(dve, xT_ready, g)
            gx = g % GROUPS
            for t in range(TG):
                i = nc.vector.tensor_scalar(xn[:, t, :], xs[:, gx * TG + t, :], mv[:, t, 0:1],
                                            rstd[:, t:t + 1], ALU.subtract, ALU.mult)
            i.then_inc(xn_ready, 1)

        def dve_xsplit(dve, g, par):
            wait(dve, xf_ready, g + 1)
            if not (isinstance(g, int) and g < 2):
                wait(dve, h0_ready, (g - 1) * UNITS)
            nc.vector.tensor_copy(x_hi[:, par, :], ps[:, XT, :]).then_inc(xhi_done, 1)
            dve.wait_ge(xhi_done, g + 1)
            nc.vector.tensor_tensor(x_lo[:, par, :], ps[:, XT, :], x_hi[:, par, :].bitcast(F32),
                                    ALU.subtract).then_inc(xsplit_ready, 1)

        def dve_top(dve, g):
            wait(dve, logits_ready, g + 1)
            nc.vector.tensor_tensor(logits[:], ps[:, LG, 0:TG * E].rearrange("p (t e) -> p t e", e=E),
                                    gb[:].unsqueeze(1).broadcast_to([P, TG, E]), ALU.add).then_inc(logits_done, 1)
            dve.wait_ge(logits_done, g + 1)
            nc.vector.memset(spare[:, 1:2], 0.0)
            for t in range(TG):
                i = nc.vector.max(top[:, t, :], logits[:, t, :])
            i.then_inc(top_done, 1)
            dve.wait_ge(top_done, g + 1)
            if not (isinstance(g, int) and g == 0):
                wait(dve, tanh_ready, g)
            nc.vector.tensor_tensor(diff[:], top[:, :, 0], top[:, :, 1], ALU.subtract).then_inc(diff_ready, 1)
            for t in range(TG):
                i = nc.vector.max_index(top_i[:, t, :], top[:, t, :], logits[:, t, :])
            i.then_inc(index_done, 1)
            dve.wait_ge(index_done, g + 1)
            nc.vector.tensor_copy(top_f[:], top_i[:, :, 0:2]).then_inc(topf_done, 1)

        def dve_gates(dve, g):
            wait(dve, tanh_ready, g + 1)
            nc.vector.tensor_scalar(w12[:, 0, :], th[:], 0.25, 0.25, ALU.mult, ALU.add)
            nc.vector.tensor_scalar(w12[:, 1, :], th[:], -0.25, 0.25, ALU.mult, ALU.add).then_inc(w12_done, 1)
            dve.wait_ge(topf_done, g + 1)
            for r in range(2):
                i = nc.vector.tensor_tensor(pick[:, r], iota[:].unsqueeze(1).broadcast_to([P, TG, E]),
                                            top_f[:, :, r:r + 1].broadcast_to([P, TG, E]), ALU.is_equal)
            i.then_inc(match_done, 1)
            dve.wait_ge(w12_done, g + 1)
            dve.wait_ge(match_done, g + 1)
            for r in range(2):
                i = nc.vector.tensor_tensor(pick[:, r], pick[:, r],
                                            w12[:, r, :].unsqueeze(2).broadcast_to([P, TG, E]), ALU.mult)
            i.then_inc(pick_done, 1)
            dve.wait_ge(pick_done, g + 1)
            if not (isinstance(g, int) and g == 0):
                wait(dve, gT_ready, g)
            nc.vector.tensor_tensor(gpad[:, :, 0:E], pick[:, 0], pick[:, 1], ALU.add).then_inc(gates_ready, 1)

        def dve_gsplit(dve, g):
            wait(dve, gf_ready, g + 1)
            if not (isinstance(g, int) and g == 0):
                wait(dve, w2_done, (g - 1) * UNITS + 1)
            nc.vector.tensor_copy(g_hi[:], ps[:, GT, :]).then_inc(ghi_done, 1)
            dve.wait_ge(ghi_done, g + 1)
            nc.vector.tensor_tensor(g_lo[:], ps[:, GT, :], g_hi[:].bitcast(F32), ALU.subtract).then_inc(gsplit_ready, 1)

        def dve_close(dve, g):
            wait(dve, yT_ready, g + 1)
            tiles = xs[:, g * TG:(g + 1) * TG, :] if isinstance(g, int) else xs[:, bass.ts(g, TG), :]
            nc.vector.tensor_tensor(tiles, tiles, ps[:, XT, :].rearrange("p (t d) -> p t d", d=P),
                                    ALU.add).then_inc(x_updated, 1)

        def dve_group(dve, g, last):
            for v in range(HEAD, UNITS + HEAD):
                if v < UNITS:
                    dve_unit(dve, g, v)
                elif not last:
                    dve_unit(dve, g + 1, v - UNITS)
                if v - 1 < UNITS:
                    dve_lo_part(dve, g, v - 1)
                elif not last:
                    dve_lo_part(dve, g + 1, v - 1 - UNITS)
                if not last:
                    if v == 5:
                        dve_xsplit(dve, g + 1, (g + 1) % 2)
                    if v == 6:
                        dve_top(dve, g + 1)
                    if v == 8:
                        dve_gates(dve, g + 1)
                    if v == 12:
                        dve_gsplit(dve, g + 1)
                    if v == 13:
                        dve_stats(dve, g + 2)
                    if v == 16:
                        dve_norm(dve, g + 2)
            dve_close(dve, g)

        @block.vector
        def _(dve):
            nc.vector.memset(gpad[:], 0.0).then_inc(gpad_zero, 1)
            dve_stats(dve, 0)
            dve_norm(dve, 0)
            dve_stats(dve, 1)
            dve_xsplit(dve, 0, 0)
            dve_norm(dve, 1)
            dve_top(dve, 0)
            dve.wait_ge(gpad_zero, 1)
            dve_gates(dve, 0)
            dve_gsplit(dve, 0)
            for u in range(HEAD):
                dve_unit(dve, 0, u)
                if u:
                    dve_lo_part(dve, 0, u - 1)
            with dve.Fori(0, GROUPS - 1) as g:
                dve_group(dve, g, False)
            dve_group(dve, GROUPS - 1, True)

        def sp_gates(sp, g):
            wait(sp, gf_ready, g + 1)
            sp.dma_start(gate_dram[g], g_f[:]).then_inc(gates_out, 16)
            sp.wait_ge(gates_out, 16 * g + 16)
            wait(sp, gated_done, (g - 1) * UNITS)
            for part, es in enumerate((slice(0, FIRST), slice(FIRST, E))):
                sp.dma_start(gates_bc[:, g % 2, es, :],
                             gate_dram[g, es].partition_broadcast(P)).then_inc(gates_in[part], 16)

        def sp_store(sp, g):
            wait(sp, x_updated, g + 1)
            for j in range(T // S):
                b = g * (T // S) + j
                sp.dma_start(out_dram[:, b], xs[:, 2 * b:2 * b + 2, :]).then_inc(stored, 16)

        @block.sync
        def _(sp):
            for g in range(GROUPS + 1):
                if g < GROUPS:
                    sp_gates(sp, g)
                if g and out_dram is not None:
                    sp_store(sp, g - 1)
            if out_dram is not None:
                sp.wait_ge(stored, 16 * NB)


def attention(nc, xs, ident, identb, wqk_hi, wqk_lo, wv_hi, wv_lo, wo_hi, wo_lo, bo_sb, eps_sb,
              neg_half, qk_dram, ps):
    NJ = 4
    HG = NH // NJ
    KP, KM = 24, 27
    SCALE = float(P // NH) ** -0.5
    SA, SBK, O, MISC = (0, 2), (4, 5), 6, 7
    with ExitStack() as c:
        def sb(n, shape, dt=F32):
            return c.enter_context(nc.sbuf_tensor(f"attn_{n}", shape, dt))

        def sem(n):
            return c.enter_context(nc.semaphore(f"attn_{n}"))

        qa = [sb(f"qa{i}", [P, NH, S], BF16) for i in range(4)]
        ka = [sb(f"ka{i}", [P, NH, S], BF16) for i in range(4)]
        va = [sb(f"va{i}", [P, 2, NH, 32]) for i in range(4)]
        ones_rows = sb("ones_rows", [3, NH * S], BF16)
        pt = sb("pt", [P, 2, NJ, 2 * S])
        stats, mv = sb("stats", [P, 2, 6]), sb("mv", [P, 2, 2])
        vare, rstd = sb("vare", [P, 2]), sb("rstd", [P, 2])
        xn = sb("xn", [P, 2, 2, HALF])
        xT = sb("xT", [P, S], F32R)
        qkp = sb("qkp", [P, 3, S], BF16)
        rem = sb("rem", [P, S])
        nm = sb("nm", [P, 2, NH])
        nmr = sb("nmr", [P, 2, NH])
        mp = sb("mp", [P, 2, 8, NH], BF16)
        mT = sb("mT", [3 * NH, S], BF16)
        spare = sb("spare", [P, 1])
        oT = sb("oT", [P, 2 * S])
        rsum = sb("rsum", [P, 2, 2, NJ])
        otok = sb("otok", [P, 2, HALF])
        osp = sb("osp", [P, 2, 2, HALF])
        oTs = sb("oTs", [P, S], F32R)

        mp_zero = sem("mp_zero")
        zeroed, ones_made, ones_in, v_init = sem("zeroed"), sem("ones_made"), sem("ones_in"), sem("v_init")
        bn_done, stats_ready, rstd_step, xn_ready = sem("bn_done"), sem("stats_ready"), sem("rstd_step"), sem("xn_ready")
        xT_ready, xhi_done, xT_split = sem("xT_ready"), sem("xhi_done"), sem("xT_split")
        proj_ready, p0_done, v_copied = sem("proj_ready"), sem("p0_done"), sem("v_copied")
        rem_done, p1_done, pieces_ready = sem("rem_done"), sem("p1_done"), sem("pieces_ready")
        pieces_out, ops_in = sem("pieces_out"), sem("ops_in")
        rows_ready, max_done = sem("rows_ready"), sem("max_done")
        m0_done, mr_done, m1_done, m_ready = sem("m0_done"), sem("mr_done"), sem("m1_done"), sem("m_ready")
        mT_ready, mT_copied, m_in = sem("mT_ready"), sem("mT_copied"), sem("m_in")
        cols_ready, exp_done, pv_done = sem("cols_ready"), sem("exp_done"), sem("pv_done")
        oT_copied, otok_ready, recip_done, norm_done = sem("oT_copied"), sem("otok_ready"), sem("recip_done"), sem("norm_done")
        ohi_done, osp_ready, oTs_ready, oTs_copied = sem("ohi_done"), sem("osp_ready"), sem("oTs_ready"), sem("oTs_copied")
        y_ready, x_updated, bias_added = sem("y_ready"), sem("x_updated"), sem("bias_added")
        block = c.enter_context(nc.Block())

        def first(v, n=1):
            return isinstance(v, int) and v < n

        def valid(b):
            return not isinstance(b, int) or 0 <= b < NB

        def run_steps(eng, step):
            for s in range(-1, 3):
                step(eng, s, s % 4)
            with eng.Fori(0, 2) as turn:
                for i in range(4):
                    step(eng, turn * 4 + (3 + i), (3 + i) % 4)
            for s in range(11, NB + 3):
                step(eng, s, s % 4)

        def misc_uses(s):
            uses = [("xT", s + 1, xT_split, s + 2), ("mT", s - 1, mT_copied, s),
                    ("project", s + 1, rem_done, s + 2), ("otok1", s - 3, norm_done, 2 * (s - 3) + 2),
                    ("oTs", s - 3, oTs_copied, s - 2), ("out", s - 3, x_updated, s - 2),
                    ("otok0", s - 2, norm_done, 2 * (s - 2) + 1)]
            return [u for u in uses if valid(u[1])]

        def misc_free(eng, s, name):
            uses = misc_uses(s - 1) + misc_uses(s)
            at = len(misc_uses(s - 1)) + [u[0] for u in misc_uses(s)].index(name)
            if at:
                _, _, semaphore, value = uses[at - 1]
                wait(eng, semaphore, value)

        def pe_cols(pe, b, sl, h):
            n = NH * b + h
            if h == 0:
                wait(pe, m_in, 48 * (b + 1))
            if not first(n, 2):
                wait(pe, exp_done, n - 1)
            for kc in range(2):
                mm = pe.matmul(ps[:, SBK[h % 2], kc * S:(kc + 1) * S], ka[sl][:, h, kc * P:(kc + 1) * P],
                               qa[sl][:, h, :], start=True, stop=True)
            mm.then_inc(cols_ready, 1)

        def pe_rows(pe, b, sl, k):
            g, qc = divmod(k, 2)
            if k == 0:
                wait(pe, ops_in, 160 * (b + 1))
            n = 8 * b + k
            if not first(n, 2):
                wait(pe, max_done, n - 1)
            for j in range(NJ):
                h = NJ * g + j
                mm = pe.matmul(ps[:, SA[k % 2] + j // 2, (j % 2) * S:(j % 2 + 1) * S],
                               qa[sl][:, h, qc * P:(qc + 1) * P], ka[sl][:, h, :], start=True, stop=True)
            mm.then_inc(rows_ready, 1)

        def pe_values(pe, b, sl, g):
            if g == 0:
                wait(pe, v_copied, b + 1)
            wait(pe, exp_done, NH * b + NJ * (g + 1))
            if g % 2 == 0 and not first(HG * b + g, 2):
                wait(pe, oT_copied, 2 * b + g // 2)
            for kc in range(2):
                for j in range(NJ):
                    mm = pe.matmul(ps[32 * j:32 * j + 32, O, (g % 2) * S:(g % 2 + 1) * S],
                                   va[sl][:, kc, NJ * g + j, :], pt[:, g % 2, j, kc * S:(kc + 1) * S],
                                   start=(kc == 0), stop=(kc == 1), tile_position=(0, 32 * j))
            mm.then_inc(pv_done, 1)

        def pe_xT(pe, b):
            wait(pe, xn_ready, b + 1)
            misc_free(pe, b - 1, "xT")
            for j in range(2):
                mm = pe.transpose(ps[:, MISC, j * P:(j + 1) * P], xn[:, j].rearrange("p a d -> p (a d)"), ident[:])
            mm.then_inc(xT_ready, 1)

        def pe_mT(pe, b):
            wait(pe, m_ready, b + 1)
            misc_free(pe, b + 1, "mT")
            for qc in range(2):
                mm = pe.transpose(ps[:, MISC, qc * HALF:(qc + 1) * HALF].bitcast(BF16),
                                  mp[:, qc].rearrange("p a h -> p (a h)"), identb[:])
            mm.then_inc(mT_ready, 1)

        def pe_project(pe, b):
            wait(pe, xT_split, b + 1)
            misc_free(pe, b - 1, "project")
            pe.matmul(ps[:, MISC, 0:S], wqk_hi[:], xT[:], start=True, stop=False, skip_group_check=True)
            pe.matmul(ps[:, MISC, 0:S], wqk_lo[:], xT[:], start=False, stop=True, skip_group_check=True)
            for j in range(2):
                o = ps[:, MISC, S + j * HALF:S + (j + 1) * HALF]
                pe.matmul(o, xT[:, j * P:(j + 1) * P], wv_hi[:], start=False, stop=False, skip_group_check=True)
                mm = pe.matmul(o, xT[:, j * P:(j + 1) * P], wv_lo[:], start=False, stop=True, skip_group_check=True)
            mm.then_inc(proj_ready, 1)

        def pe_otok(pe, b, pair):
            wait(pe, oT_copied, 2 * b + pair + 1)
            misc_free(pe, b + 3 if pair else b + 2, "otok1" if pair else "otok0")
            for g in range(2):
                for qc in range(2):
                    mm = pe.transpose(ps[:, MISC, (2 * qc + g) * P:(2 * qc + g + 1) * P],
                                      oT[:, g * S + qc * P:g * S + (qc + 1) * P], ident[:])
            mm.then_inc(otok_ready, 1)

        def pe_oTs(pe, b):
            wait(pe, osp_ready, b + 1)
            misc_free(pe, b + 3, "oTs")
            for qc in range(2):
                mm = pe.transpose(ps[:, MISC, qc * P:(qc + 1) * P], osp[:, qc].rearrange("p a d -> p (a d)"), ident[:])
            mm.then_inc(oTs_ready, 1)

        def pe_out(pe, b):
            wait(pe, oTs_copied, b + 1)
            misc_free(pe, b + 3, "out")
            for qc in range(2):
                o = ps[:, MISC, qc * P:(qc + 1) * P]
                pe.matmul(o, oTs[:, qc * P:(qc + 1) * P], wo_hi[:], start=True, stop=False)
                mm = pe.matmul(o, oTs[:, qc * P:(qc + 1) * P], wo_lo[:], start=False, stop=True)
            mm.then_inc(y_ready, 1)

        def pe_step(pe, s, sl):
            for k in range(2 * HG):
                if valid(s - 2):
                    pe_cols(pe, s - 2, (sl - 2) % 4, 2 * k)
                    pe_cols(pe, s - 2, (sl - 2) % 4, 2 * k + 1)
                if k == 0 and valid(s + 1):
                    pe_xT(pe, s + 1)
                if k == 1 and valid(s - 1):
                    pe_mT(pe, s - 1)
                if k == 2 and valid(s + 1):
                    pe_project(pe, s + 1)
                if k == 3 and valid(s - 3):
                    pe_otok(pe, s - 3, 1)
                if k == 5 and valid(s - 3):
                    pe_oTs(pe, s - 3)
                if k == 6 and valid(s - 3):
                    pe_out(pe, s - 3)
                if k == 7 and valid(s - 2):
                    pe_otok(pe, s - 2, 0)
                if valid(s):
                    pe_rows(pe, s, sl, k)
                if k == 1 and valid(s - 3):
                    pe_values(pe, s - 3, (sl - 3) % 4, 3)
                if k in (3, 5, 7) and valid(s - 2):
                    pe_values(pe, s - 2, (sl - 2) % 4, (k - 3) // 2)

        @block.tensor
        def _(pe):
            wait(pe, v_init, 8)
            wait(pe, zeroed, 8)
            wait(pe, ones_in, 4 * 16)
            run_steps(pe, pe_step)

        def act_exp(act, b, h):
            g, j = divmod(h, NJ)
            if j == 0 and not first(HG * b + g, 2):
                wait(act, pv_done, HG * b + g - 1)
            wait(act, cols_ready, NH * b + h + 1)
            nc.scalar.activation(pt[:, g % 2, j, :], ps[:, SBK[h % 2], :], ACT.Exp, scale=SCALE).then_inc(exp_done, 1)

        def act_xhi(act, b):
            wait(act, xT_ready, b + 1)
            if not first(b):
                wait(act, proj_ready, b)
            nc.scalar.activation(xT[:], ps[:, MISC, 0:S], ACT.Copy).then_inc(xhi_done, 1)

        def act_mT(act, b):
            wait(act, mT_ready, b + 1)
            if not first(b):
                wait(act, m_in, 48 * b)
            nc.scalar.activation(mT[:], ps[0:3 * NH, MISC, 0:P].bitcast(BF16), ACT.Copy).then_inc(mT_copied, 1)

        def act_project(act, b, sl):
            wait(act, proj_ready, b + 1)
            if not first(b):
                wait(act, pieces_out, 32 * b)
            nc.scalar.activation(qkp[:, 0, :], ps[:, MISC, 0:S], ACT.Copy).then_inc(p0_done, 1)
            if not first(b, 4):
                wait(act, pv_done, HG * (b - 3))
            nc.scalar.activation(va[sl][:, :, :, 0:DH],
                                 ps[:, MISC, S:S + 2 * HALF].rearrange("p (c h d) -> p c h d", c=2, d=DH),
                                 ACT.Copy).then_inc(v_copied, 1)

        def act_oT(act, b, pair):
            wait(act, pv_done, HG * b + 2 * pair + 2)
            if not first(2 * b + pair):
                wait(act, otok_ready, 2 * b + pair)
            nc.scalar.activation(oT[:], ps[:, O, :], ACT.Copy).then_inc(oT_copied, 1)

        def act_oTs(act, b):
            wait(act, oTs_ready, b + 1)
            if not first(b):
                wait(act, y_ready, b)
            nc.scalar.activation(oTs[:], ps[:, MISC, 0:S], ACT.Copy).then_inc(oTs_copied, 1)

        def act_step(act, s, sl):
            for k in range(2 * HG):
                if k == 2 and valid(s - 3):
                    act_oT(act, s - 3, 1)
                if k == 6 and valid(s - 2):
                    act_oT(act, s - 2, 0)
                if valid(s - 2):
                    act_exp(act, s - 2, 2 * k)
                    act_exp(act, s - 2, 2 * k + 1)
                if k == 0 and valid(s + 1):
                    act_xhi(act, s + 1)
                if k == 1 and valid(s - 1):
                    act_mT(act, s - 1)
                if k == 2 and valid(s + 1):
                    act_project(act, s + 1, (sl + 1) % 4)
                if k == 5 and valid(s - 3):
                    act_oTs(act, s - 3)

        @block.scalar
        def _(act):
            wait(act, v_init, 8)
            run_steps(act, act_step)

        def pool_rstd(pool, b):
            wait(pool, stats_ready, b + 1)
            nc.gpsimd.tensor_tensor(vare[:], mv[:, :, 1], eps_sb[:, 0:2], ALU.add).then_inc(rstd_step, 1)
            pool.wait_ge(rstd_step, 2 * b + 1)
            nc.gpsimd.tensor_tensor(rstd[:], vare[:], neg_half[:, 0:2], ALU.pow).then_inc(rstd_step, 1)

        def tiles(b):
            return xs[:, 2 * b:2 * b + 2, :] if isinstance(b, int) else xs[:, bass.ts(b, 2), :]

        def pool_bias(pool, b):
            wait(pool, xn_ready, b + 1)
            nc.gpsimd.tensor_tensor(tiles(b), tiles(b), bo_sb[:].unsqueeze(1).broadcast_to([P, 2, P]),
                                    ALU.add).then_inc(bias_added, 1)

        def pool_step(pool, s, sl):
            if valid(s + 2):
                pool_rstd(pool, s + 2)
                pool_bias(pool, s + 2)

        @block.gpsimd
        def _(pool):
            pool.memset(ones_rows[:], 1.0).then_inc(ones_made, 1)
            for i in range(4):
                pool.memset(va[i][:], 0.0).then_inc(v_init, 1)
            for i in range(4):
                pool.wait_ge(v_init, 4 + i)
                pool.memset(va[i][:, :, :, DH:DH + 1], 1.0).then_inc(v_init, 1)
            pool_step(pool, -2, 0)
            run_steps(pool, pool_step)

        def dve_stats(dve, b):
            if not first(b):
                wait(dve, xn_ready, b)
            for j in range(2):
                i = nc.vector.bn_stats(stats[:, j, :], xs[:, 2 * b + j, :])
            i.then_inc(bn_done, 1)
            wait(dve, bn_done, b + 1)
            nc.vector.memset(spare[:], 0.0)
            for j in range(2):
                i = nc.vector.bn_aggr(mv[:, j, :], stats[:, j, :])
            i.then_inc(stats_ready, 1)

        def dve_norm(dve, b):
            wait(dve, rstd_step, 2 * b + 2)
            if not first(b):
                wait(dve, xT_ready, b)
            for j in range(2):
                i = nc.vector.tensor_scalar(xn[:, j], xs[:, 2 * b + j, 0:HALF].unsqueeze(1).broadcast_to([P, 2, HALF]),
                                            mv[:, j, 0:1], rstd[:, j:j + 1], ALU.subtract, ALU.mult)
            i.then_inc(xn_ready, 1)

        def dve_xlo(dve, b):
            wait(dve, xhi_done, b + 1)
            nc.vector.tensor_tensor(xT[HALF:P, :], ps[HALF:P, MISC, 0:S], xT[HALF:P, :].bitcast(F32),
                                    ALU.subtract).then_inc(xT_split, 1)

        def dve_pieces(dve, b):
            wait(dve, v_copied, b + 1)
            nc.vector.tensor_tensor(rem[:], ps[:, MISC, 0:S], qkp[:, 0, :], ALU.subtract).then_inc(rem_done, 1)
            wait(dve, rem_done, b + 1)
            nc.vector.tensor_copy(qkp[:, 1, :], rem[:]).then_inc(p1_done, 1)
            wait(dve, p1_done, b + 1)
            nc.vector.tensor_tensor(qkp[:, 2, :], rem[:], qkp[:, 1, :], ALU.subtract).then_inc(pieces_ready, 1)

        def dve_max(dve, b, k):
            g, qc = divmod(k, 2)
            wait(dve, rows_ready, 8 * b + k + 1)
            if k == 0 and first(b):
                dve.wait_ge(mp_zero, 1)
            elif k == 0:
                wait(dve, m_ready, b)
            nc.vector.tensor_reduce(nm[:, qc, NJ * g:NJ * g + NJ],
                                    ps[:, SA[k % 2]:SA[k % 2] + 2, :].rearrange("p c (j t) -> p (c j) t", t=S),
                                    AX.X, ALU.max, negate=True).then_inc(max_done, 1)

        def dve_m(dve, b):
            wait(dve, max_done, 8 * b + 8)
            if not first(b):
                wait(dve, mT_ready, b)
            nc.vector.tensor_copy(mp[:, :, 0, :], nm[:]).then_inc(m0_done, 1)
            wait(dve, m0_done, b + 1)
            nc.vector.tensor_tensor(nmr[:], nm[:], mp[:, :, 0, :], ALU.subtract).then_inc(mr_done, 1)
            wait(dve, mr_done, b + 1)
            nc.vector.tensor_copy(mp[:, :, 1, :], nmr[:]).then_inc(m1_done, 1)
            wait(dve, m1_done, b + 1)
            nc.vector.tensor_tensor(mp[:, :, 2, :], nmr[:], mp[:, :, 1, :], ALU.subtract).then_inc(m_ready, 1)

        def dve_otok(dve, b, pair):
            n = 2 * b + pair
            wait(dve, otok_ready, n + 1)
            o = ps[:, MISC, :].rearrange("p (c h k) -> p c h k", c=2, k=32)
            if not first(n):
                wait(dve, norm_done, n)
            nc.vector.reciprocal(rsum[:].rearrange("p c g j -> p c (g j)"), o[:, :, :, DH]).then_inc(recip_done, 1)
            wait(dve, recip_done, n + 1)
            if pair == 0 and not first(b):
                wait(dve, osp_ready, b)
            nc.vector.tensor_tensor(
                otok[:, :, pair * 32:pair * 32 + 32].rearrange("p c (h d) -> p c h d", d=DH), o[:, :, :, 0:DH],
                rsum[:].rearrange("p c g j -> p c (g j)").unsqueeze(3).broadcast_to([P, 2, 2 * NJ, DH]),
                ALU.mult).then_inc(norm_done, 1)

        def dve_osplit(dve, b):
            wait(dve, norm_done, 2 * b + 2)
            if not first(b):
                wait(dve, oTs_ready, b)
            nc.vector.tensor_copy(osp[:, :, 0, :].bitcast(F32R), otok[:]).then_inc(ohi_done, 1)
            wait(dve, ohi_done, b + 1)
            nc.vector.tensor_tensor(osp[:, :, 1, :], otok[:], osp[:, :, 0, :], ALU.subtract).then_inc(osp_ready, 1)

        def dve_residual(dve, b):
            wait(dve, y_ready, b + 1)
            wait(dve, bias_added, b + 1)
            t = tiles(b)
            nc.vector.tensor_tensor(t, t, ps[:, MISC, 0:S].rearrange("p (t d) -> p t d", d=P), ALU.add).then_inc(x_updated, 1)

        def dve_step(dve, s, sl):
            for k in range(2 * HG):
                if valid(s):
                    dve_max(dve, s, k)
                if k == 0 and valid(s + 1):
                    dve_xlo(dve, s + 1)
                if k == 2 and valid(s + 1):
                    dve_pieces(dve, s + 1)
                if k == 3 and valid(s - 3):
                    dve_otok(dve, s - 3, 1)
                    dve_osplit(dve, s - 3)
                if k == 4 and valid(s + 2):
                    dve_stats(dve, s + 2)
                if k == 6 and valid(s + 2):
                    dve_norm(dve, s + 2)
                if k == 6 and valid(s - 3):
                    dve_residual(dve, s - 3)
                if k == 7 and valid(s - 2):
                    dve_otok(dve, s - 2, 0)
                if k == 7 and valid(s):
                    dve_m(dve, s)

        @block.vector
        def _(dve):
            dve.memset(mp[:], 0.0).then_inc(mp_zero, 1)
            for i in range(4):
                dve.memset(qa[i][:].bitcast(U32), 0).then_inc(zeroed, 1)
                dve.memset(ka[i][:].bitcast(U32), 0).then_inc(zeroed, 1)
            dve_stats(dve, 0)
            dve_norm(dve, 0)
            run_steps(dve, dve_step)

        def sp_pieces(sp, b):
            wait(sp, pieces_ready, b + 1)
            if not first(b, 4):
                wait(sp, cols_ready, NH * (b - 3))
            for i in range(2):
                sp.dma_start(qk_dram[b, i].rearrange("a c t -> c a t"), qkp[i * HALF:(i + 1) * HALF]).then_inc(pieces_out, 16)

        def sp_operands(sp, b, sl):
            wait(sp, pieces_out, 32 * (b + 1))
            q = qk_dram[b, 0].rearrange("a (d h) t -> a d (h t)", d=DH)
            k = qk_dram[b, 1].rearrange("a (d h) t -> a d (h t)", d=DH)
            qv, kv = (t[sl][:].rearrange("p h t -> p (h t)") for t in (qa, ka))
            for r, piece in enumerate((0, 0, 0, 1, 1, 2)):
                sp.dma_start(qv[DH * r:DH * r + DH, :], q[piece]).then_inc(ops_in, 16)
            r = 0
            for n in (3, 2, 1):
                sp.dma_start(kv[r:r + n * DH, :], k[0:n].rearrange("a d t -> (a d) t")).then_inc(ops_in, 16)
                r += n * DH
            sp.dma_start(qv[KP:KM, :], qv[P - 3:P, :]).then_inc(ops_in, 16)

        def sp_max(sp, b, sl):
            wait(sp, mT_copied, b + 1)
            for i in range(3):
                sp.dma_start(qa[sl][KP + i:KP + i + 1], mT[NH * i:NH * i + NH, :]).then_inc(m_in, 16)

        def sp_step(sp, s, sl):
            if valid(s - 1):
                sp_max(sp, s - 1, (sl - 1) % 4)
            if valid(s + 1):
                sp_pieces(sp, s + 1)
                sp_operands(sp, s + 1, (sl + 1) % 4)

        @block.sync
        def _(sp):
            sp.wait_ge(ones_made, 1)
            sp.wait_ge(zeroed, 8)
            for i in range(4):
                sp.dma_start(ka[i][KP:KM].rearrange("p h t -> p (h t)"), ones_rows[:]).then_inc(ones_in, 16)
            for s in range(-1, NB + 3):
                sp_step(sp, s, s % 4)


def kernel(L0_attn_x, L0_attn_Wq, L0_attn_Wk, L0_attn_Wv, L0_attn_Wo, L0_attn_bo, L0_ffn_gate_w,
           L0_ffn_gate_b, L0_ffn_w0, L0_ffn_b0, L0_ffn_w1, L0_ffn_b1, L0_ffn_w2, L0_ffn_b2):
    import numpy as np
    import concourse.bacc as bacc
    from concourse import mybir as mb
    from concourse.bass_utils import run_bass_kernel_spmd

    def np32(a):
        return np.asarray(a)

    def head_minor(w):
        return np32(w).reshape(NH, DH, HALF).transpose(1, 0, 2).reshape(HALF, HALF)

    arrays = {
        "x": np32(L0_attn_x),
        "gate_wT": np32(L0_ffn_gate_w).T,
        "gate_b": np32(L0_ffn_gate_b).reshape(E),
        "w0T": np32(L0_ffn_w0).transpose(2, 0, 1).reshape(P, E * HID),
        "b0T": np32(L0_ffn_b0).reshape(UNITS, P).T,
        "w1T": np32(L0_ffn_w1).transpose(2, 0, 1).reshape(P, E * HID),
        "b1T": np32(L0_ffn_b1).reshape(UNITS, P).T,
        "w2T": np32(L0_ffn_w2).reshape(E, P, CH, P).transpose(3, 0, 2, 1).reshape(P, E * HID),
        "b2": np32(L0_ffn_b2),
        "wqT": head_minor(L0_attn_Wq).T,
        "wkT": head_minor(L0_attn_Wk).T,
        "wvT": np32(L0_attn_Wv).T,
        "woT": np32(L0_attn_Wo).T,
        "bo": np32(L0_attn_bo),
    }
    arrays = {k: np.ascontiguousarray(v) for k, v in arrays.items()}
    nc = bacc.Bacc("TRN2", target_bir_lowering=False, num_devices=1)
    aps = {k: nc.dram_tensor(k, v.shape, F32, kind="ExternalInput").ap() for k, v in arrays.items()}
    out = nc.dram_tensor("out", (NB, S, P), F32, kind="ExternalOutput").ap()
    macaron(nc, **aps, out=out)
    r = run_bass_kernel_spmd(nc, [arrays], core_ids=[0])
    return r.results[0]["out"]
```

```python
from contextlib import ExitStack

import concourse.bass as bass
from concourse import mybir

ALU = mybir.AluOpType
ACT = mybir.ActivationFunctionType
AX = mybir.AxisListType
F32 = mybir.dt.float32
F32R = mybir.dt.float32r
BF16 = mybir.dt.bfloat16
U32 = mybir.dt.uint32

P = 128
NB, S = 16, 256
TILES = NB * S // P
E, HID = 8, 256
CH = HID // P
T = 512
TG = T // P
GROUPS = NB * S // T
UNITS = E * CH
NH, DH, HALF = 16, 4, 64
EPS = 1e-5
FIRST = 2
LAG = 3
HEAD = LAG + 1


def wait(eng, sem, value):
    if isinstance(value, int) and value <= 0:
        return
    eng.wait_ge(sem, value)


def macaron(nc, x, gate_wT, gate_b, w0T, b0T, w1T, b1T, w2T, b2, wqT, wkT, wvT, woT, bo, out):
    x_dram = x.rearrange("b (p j) d -> p b j d", j=2)
    out_dram = out.rearrange("b (p j) d -> p b j d", j=2)
    kq_dram = nc.dram_tensor("kq_pieces", [NB, 4, 2, HALF, S], BF16)
    gate_dram = nc.dram_tensor("gates", [2, GROUPS, E, T], F32)

    with ExitStack() as ctx:
        def sb(name, shape, dt=F32, c=ctx):
            return c.enter_context(nc.sbuf_tensor(name, shape, dt))

        xs = sb("x_tokens", [P, TILES, P])
        ident = sb("ident", [P, P])
        identb = sb("identb", [P, P], BF16)
        w_hi = [sb(f"w{i}_hi", [P, E * HID], F32R) for i in range(3)]
        w_lo = [sb(f"w{i}_lo", [P, E * HID], F32R) for i in range(3)]
        b2_hi, b2_lo = sb("b2_hi", [P, P], F32R), sb("b2_lo", [P, P], F32R)
        wqk_hi, wqk_lo = sb("wqk_hi", [P, P], F32R), sb("wqk_lo", [P, P], F32R)
        wv_hi, wv_lo = sb("wv_hi", [P, HALF], F32R), sb("wv_lo", [P, HALF], F32R)
        wo_hi, wo_lo = sb("wo_hi", [P, P], F32R), sb("wo_lo", [P, P], F32R)
        gw = sb("gate_w_sb", [P, E])
        gb = sb("gate_b_sb", [P, E])
        bias0 = sb("bias0", [P, UNITS])
        bias1 = sb("bias1", [P, UNITS])
        bo_sb = sb("bo_sb", [P, P])
        iota = sb("iota", [P, E])
        neg_half = sb("neg_half", [P, TG])
        eps_sb = sb("eps_sb", [P, TG])
        ps = ctx.enter_context(nc.psum_tensor("ps", [P, 8, T], F32))

        weights = (w_hi, w_lo, b2_hi, b2_lo, gw, gb, bias0, bias1, iota, neg_half, eps_sb)
        dram = dict(w0=w0T, w1=w1T, w2=w2T, b2=b2, wq=wqT, wk=wkT, wv=wvT, wo=woT, bo=bo,
                    gate_w=gate_wT, gate_b=gate_b, b0=b0T, b1=b1T, x=x_dram)
        attn_weights = (wqk_hi, wqk_lo, wv_hi, wv_lo, wo_hi, wo_lo, bo_sb, identb)
        ffn(nc, "ffn1", xs, ident, weights, gate_dram[0], ps, None, (dram, attn_weights))
        attention(nc, xs, ident, identb, wqk_hi, wqk_lo, wv_hi, wv_lo, wo_hi, wo_lo, bo_sb,
                  eps_sb, neg_half, kq_dram, ps)
        ffn(nc, "ffn2", xs, ident, weights, gate_dram[1], ps, out_dram, None)


def ffn(nc, name, xs, ident, weights, gate_dram, ps, out_dram, load):
    w_hi, w_lo, b2_hi, b2_lo, gw, gb, bias0, bias1, iota, neg_half, eps_sb = weights
    H1, H0, Y, XT, LG, GT = (0, 1), (2, 3), 4, 5, 6, 7
    with ExitStack() as c:
        def sb(n, shape, dt=F32):
            return c.enter_context(nc.sbuf_tensor(f"{name}_{n}", shape, dt))

        def sem(n):
            return c.enter_context(nc.semaphore(f"{name}_{n}"))

        gates_bc = sb("gates_bc", [P, 2, E, T])
        stats, mv = sb("stats", [P, TG, 6]), sb("mv", [P, TG, 2])
        vare, rstd = sb("vare", [P, TG]), sb("rstd", [P, TG])
        xn = sb("xn", [P, TG, P])
        xf = sb("xf", [P, T])
        x_hi, x_lo = sb("x_hi", [P, 2, T], F32R), sb("x_lo", [P, 2, T], F32R)
        logits, top = sb("logits", [P, TG, E]), sb("top", [P, TG, E])
        top_i, top_f = sb("top_i", [P, TG, E], U32), sb("top_f", [P, TG, 2])
        diff, th, w12 = sb("diff", [P, TG]), sb("th", [P, TG]), sb("w12", [P, 2, TG])
        pick = sb("pick", [P, 2, TG, E])
        gpad = sb("gpad", [P, TG, P])
        g_hi, g_lo, g_f = sb("g_hi", [P, T], F32R), sb("g_lo", [P, T], F32R), sb("g_f", [E, T])
        silu = sb("silu", [P, 2, T])
        gated = sb("gated", [P, 2, T])
        act_sb = sb("act", [P, 4, T])
        act_hi, act_lo = sb("act_hi", [P, 4, T], F32R), sb("act_lo", [P, 4, T], F32R)
        y_sb = sb("y_sb", [P, T])
        spare = sb("spare", [P, 2])
        if load:
            stage = [sb(f"stage{i}", [P, E * HID]) for i in range(3)]
            b2_f, wqk_f, wv_f, wo_f = sb("b2_f", [P, P]), sb("wqk_f", [P, P]), sb("wv_f", [P, HALF]), sb("wo_f", [P, P])
            iota_i = sb("iota_i", [P, E], mybir.dt.int32)
            dram, (wqk_hi, wqk_lo, wv_hi, wv_lo, wo_hi, wo_lo, bo_sb, identb) = load
            b2_part = (b2_f[:], b2_hi[:], b2_lo[:], [sem("b2_loaded"), 1])
            parts, part_at = [], {}
            for q in range(E // 2):
                cols = slice(q * 2 * HID, (q + 1) * 2 * HID)
                for w in (1, 0, 2):
                    if (w, q) == (2, 0):
                        parts.append(b2_part)
                    parts.append((stage[w][:, cols], w_hi[w][:, cols], w_lo[w][:, cols], [sem(f"w{w}_{q}_loaded"), 1]))
                    part_at[w, q] = len(parts)
            attn_loaded = sem("attn_weights_loaded")
            for f, h, l in ((wqk_f, wqk_hi, wqk_lo), (wv_f, wv_hi, wv_lo), (wo_f, wo_hi, wo_lo)):
                parts.append((f[:], h[:], l[:], [attn_loaded, 9]))
            x_loaded = [sem("x0_loaded"), sem("x1_loaded"), sem("x_rest_loaded")]
            router_loaded = sem("router_loaded")
            const_loaded, const_made, whi_done = sem("const_loaded"), sem("const_made"), sem("whi_done")
            early_split, split_done = sem("early_split"), sem("split_done")
            b2_zero, ident_step = sem("b2_zero"), sem("ident_step")
        EARLY = 4

        stats_ready, rstd_step, xn_ready = sem("stats_ready"), sem("rstd_step"), sem("xn_ready")
        xT_ready, xf_ready, xsplit_ready = sem("xT_ready"), sem("xf_ready"), sem("xsplit_ready")
        logits_ready, diff_ready, tanh_ready = sem("logits_ready"), sem("diff_ready"), sem("tanh_ready")
        gates_ready, gT_ready, gf_ready = sem("gates_ready"), sem("gT_ready"), sem("gf_ready")
        gsplit_ready, gates_out, gates_in = sem("gsplit_ready"), sem("gates_out"), (sem("gates_in_first"), sem("gates_in_rest"))
        h1_ready, h0_ready, silu_done = sem("h1_ready"), sem("h0_ready"), sem("silu_done")
        gated_done, act_done, hi_done, lo_done = sem("gated_done"), sem("act_done"), sem("hi_done"), sem("lo_done")
        w2_done = sem("w2_done")
        y_ready, y_copied, yT_ready = sem("y_ready"), sem("y_copied"), sem("yT_ready")
        x_updated, stored = sem("x_updated"), sem("stored")
        bn_done, xhi_done, logits_done, top_done = sem("bn_done"), sem("xhi_done"), sem("logits_done"), sem("top_done")
        index_done, topf_done, w12_done = sem("index_done"), sem("topf_done"), sem("w12_done")
        match_done, pick_done, ghi_done, gpad_zero = sem("match_done"), sem("pick_done"), sem("ghi_done"), sem("gpad_zero")
        block = c.enter_context(nc.Block())

        def split_upto(pe, count):
            if count <= EARLY:
                pe.wait_ge(early_split, count)
            else:
                pe.wait_ge(split_done, count - EARLY)

        def pe_first(pe, g, u, par):
            e, k = divmod(u, CH)
            cols = slice(e * HID + k * P, e * HID + k * P + P)
            U = g * UNITS + u
            if u == 0:
                wait(pe, xsplit_ready, g + 1)
            if load and isinstance(g, int) and g == 0 and u % (2 * CH) == 0:
                split_upto(pe, part_at[0, u // (2 * CH)])
            for bank, w, ready, free in ((H1[u % 2], 1, h1_ready, silu_done),
                                         (H0[u % 2], 0, h0_ready, act_done)):
                if not (isinstance(U, int) and U < 2):
                    wait(pe, free, U - 1)
                o = ps[:, bank, :]
                pe.matmul(o, w_hi[w][:, cols], x_hi[:, par, :], start=True, stop=False)
                pe.matmul(o, w_hi[w][:, cols], x_lo[:, par, :], start=False, stop=False)
                pe.matmul(o, w_lo[w][:, cols], x_hi[:, par, :], start=False, stop=True).then_inc(ready, 1)

        def pe_second(pe, g, u):
            U = g * UNITS + u
            o = ps[:, Y, :]
            if load and isinstance(g, int) and g == 0 and u % (2 * CH) == 0:
                split_upto(pe, part_at[2, u // (2 * CH)])
            if u == 0:
                wait(pe, gsplit_ready, g + 1)
                if not (isinstance(g, int) and g == 0):
                    wait(pe, y_copied, g)
                pe.matmul(o, b2_hi[:], g_hi[:], start=True, stop=False)
                pe.matmul(o, b2_hi[:], g_lo[:], start=False, stop=False)
                pe.matmul(o, b2_lo[:], g_hi[:], start=False, stop=False)
            ws = slice(u * P, u * P + P)
            wait(pe, hi_done, U + 1)
            pe.matmul(o, w_hi[2][:, ws], act_hi[:, u % 4, :], start=False, stop=False)
            pe.matmul(o, w_lo[2][:, ws], act_hi[:, u % 4, :], start=False, stop=False)
            wait(pe, lo_done, U + 1)
            mm = pe.matmul(o, w_hi[2][:, ws], act_lo[:, u % 4, :], start=False, stop=(u == UNITS - 1))
            mm.then_inc(w2_done, 1)

        def pe_norm(pe, g):
            wait(pe, xn_ready, g + 1)
            wait(pe, xsplit_ready, g)
            for t in range(TG):
                mm = pe.transpose(ps[:, XT, t * P:(t + 1) * P], xn[:, t, :], ident[:])
            mm.then_inc(xT_ready, 1)

        def pe_logits(pe, g):
            wait(pe, xf_ready, g + 1)
            for t in range(TG):
                mm = pe.matmul(ps[:, LG, t * E:(t + 1) * E], xf[:, t * P:(t + 1) * P], gw[:], start=True, stop=True)
            mm.then_inc(logits_ready, 1)

        def pe_gates(pe, g):
            wait(pe, gates_ready, g + 1)
            if not (isinstance(g, int) and g < 2):
                wait(pe, x_updated, g - 1)
            for t in range(TG):
                mm = pe.transpose(ps[:, GT, t * P:(t + 1) * P], gpad[:, t, :], ident[:])
            mm.then_inc(gT_ready, 1)

        def pe_close(pe, g):
            wait(pe, y_copied, g + 1)
            wait(pe, gsplit_ready, (g + 2) if not (isinstance(g, int) and g == GROUPS - 1) else g + 1)
            for t in range(TG):
                mm = pe.transpose(ps[:, GT, t * P:(t + 1) * P], y_sb[:, t * P:(t + 1) * P], ident[:])
            mm.then_inc(yT_ready, 1)

        def pe_group(pe, g, last):
            par, nxt = g % 2, (g + 1) % 2
            for v in range(HEAD, UNITS + HEAD):
                if v < UNITS:
                    pe_first(pe, g, v, par)
                elif not last:
                    pe_first(pe, g + 1, v - UNITS, nxt)
                if v == HEAD:
                    if not (isinstance(g, int) and g == 0):
                        pe_close(pe, g - 1)
                    pe_second(pe, g, 0)
                if v - LAG < UNITS:
                    pe_second(pe, g, v - LAG)
                if not last:
                    if v == 4:
                        pe_norm(pe, g + 1)
                    if v == 6:
                        pe_logits(pe, g + 1)
                    if v == 11:
                        pe_gates(pe, g + 1)
            if last:
                pe_close(pe, g)

        @block.tensor
        def _(pe):
            if load:
                pe.wait_ge(ident_step, 3)
            pe_norm(pe, 0)
            if load:
                pe.wait_ge(router_loaded, 2 * 16)
            pe_logits(pe, 0)
            if load:
                pe_gates(pe, 0)
            for u in range(2):
                pe_first(pe, 0, u, 0)
            if not load:
                pe_gates(pe, 0)
            for u in range(2, HEAD):
                pe_first(pe, 0, u, 0)
            pe_group(pe, 0, False)
            with pe.Fori(1, GROUPS - 1) as g:
                pe_group(pe, g, False)
            pe_group(pe, GROUPS - 1, True)

        def act_unit(act, g, u):
            U = g * UNITS + u
            wait(act, h1_ready, U + 1)
            if not (isinstance(U, int) and U < 2):
                wait(act, gated_done, U - 1)
            nc.scalar.activation(silu[:, u % 2, :], ps[:, H1[u % 2], :], ACT.Silu,
                                 bias=bias1[:, u:u + 1]).then_inc(silu_done, 1)

        def act_hi_part(act, g, u):
            U = g * UNITS + u
            wait(act, act_done, U + 1)
            if not (isinstance(U, int) and U < 4):
                wait(act, w2_done, U - 3)
            nc.scalar.activation(act_hi[:, u % 4, :], act_sb[:, u % 4, :], ACT.Copy).then_inc(hi_done, 1)

        def act_xf(act, g):
            wait(act, xT_ready, g + 1)
            if not (isinstance(g, int) and g == 0):
                wait(act, logits_ready, g)
            nc.scalar.activation(xf[:], ps[:, XT, :], ACT.Copy).then_inc(xf_ready, 1)

        def act_tanh(act, g):
            wait(act, diff_ready, g + 1)
            nc.scalar.activation(th[:], diff[:], ACT.Tanh, scale=0.5).then_inc(tanh_ready, 1)

        def act_gf(act, g):
            wait(act, gT_ready, g + 1)
            if not (isinstance(g, int) and g == 0):
                wait(act, gates_out, g * 16)
            nc.scalar.activation(g_f[:], ps[0:E, GT, :], ACT.Copy).then_inc(gf_ready, 1)

        def act_y(act, g):
            wait(act, w2_done, (g + 1) * UNITS)
            if not (isinstance(g, int) and g == 0):
                wait(act, yT_ready, g)
            nc.scalar.activation(y_sb[:], ps[:, Y, :], ACT.Copy).then_inc(y_copied, 1)

        def act_split(act, k):
            if k < len(parts):
                full, hi, _, (loaded, count) = parts[k]
                act.wait_ge(loaded, 16 * count)
                nc.scalar.activation(hi, full, ACT.Copy).then_inc(whi_done, 1)

        def act_load(act):
            act.dma_start(xv(0), dram["x"][:, 0:2]).then_inc(x_loaded[0], 16)
            act.dma_start(gw[:], dram["gate_w"]).then_inc(router_loaded, 16)
            act.dma_start(gb[:], dram["gate_b"].partition_broadcast(P)).then_inc(router_loaded, 16)
            for dst, n in ((bias0[:], "b0"), (bias1[:], "b1")):
                act.dma_start(dst, dram[n]).then_inc(const_loaded, 16)

        def xv(g):
            return xs[:, g * TG:(g + 1) * TG, :].rearrange("p (b j) d -> p b j d", j=2)

        def act_group(act, g, last):
            for v in range(HEAD, UNITS + HEAD):
                if v == UNITS + LAG:
                    act_y(act, g)
                if v < UNITS:
                    act_unit(act, g, v)
                elif not last:
                    act_unit(act, g + 1, v - UNITS)
                if v - 1 < UNITS:
                    act_hi_part(act, g, v - 1)
                elif not last:
                    act_hi_part(act, g + 1, v - 1 - UNITS)
                if load and isinstance(g, int) and g == 0 and v < UNITS:
                    act_split(act, v + EARLY - 1)
                if not last:
                    if v == 5:
                        act_xf(act, g + 1)
                    if v == 9:
                        act_tanh(act, g + 1)
                    if v == 12:
                        act_gf(act, g + 1)

        @block.scalar
        def _(act):
            if load:
                act_load(act)
            act_xf(act, 0)
            if load:
                for k in range(EARLY):
                    act_split(act, k)
            act_tanh(act, 0)
            act_gf(act, 0)
            if load:
                act.wait_ge(const_loaded, 2 * 16)
            for u in range(HEAD):
                act_unit(act, 0, u)
                if u:
                    act_hi_part(act, 0, u - 1)
                    if load:
                        act_split(act, EARLY + u - 1)
            act_group(act, 0, False)
            with act.Fori(1, GROUPS - 1) as g:
                act_group(act, g, False)
            act_group(act, GROUPS - 1, True)

        def pool_unit(pool, g, u, par):
            U = g * UNITS + u
            if not (isinstance(U, int) and U < 2):
                wait(pool, act_done, U - 1)
            if u in (0, FIRST * CH):
                wait(pool, gates_in[u > 0], (g + 1) * 16)
            wait(pool, silu_done, U + 1)
            nc.gpsimd.tensor_tensor(gated[:, u % 2, :], silu[:, u % 2, :], gates_bc[:, par, u // CH, :],
                                    ALU.mult).then_inc(gated_done, 1)

        def pool_rstd(pool, g):
            wait(pool, stats_ready, g + 1)
            nc.gpsimd.tensor_tensor(vare[:], mv[:, :, 1], eps_sb[:], ALU.add).then_inc(rstd_step, 1)
            pool.wait_ge(rstd_step, 2 * g + 1)
            nc.gpsimd.tensor_tensor(rstd[:], vare[:], neg_half[:], ALU.pow).then_inc(rstd_step, 1)

        def pool_group(pool, g, par, last):
            for v in range(HEAD, UNITS + HEAD):
                if v < UNITS:
                    pool_unit(pool, g, v, par)
                elif not last:
                    pool_unit(pool, g + 1, v - UNITS, 1 - par)
                if v == 15 and not last:
                    pool_rstd(pool, g + 2)

        @block.gpsimd
        def _(pool):
            if load:
                nc.gpsimd.memset(ident[:], 0.0).then_inc(ident_step, 1)
                nc.gpsimd.iota(iota_i[:], pattern=[[1, E]], base=0, channel_multiplier=0).then_inc(ident_step, 1)
                pool.wait_ge(ident_step, 2)
                nc.gpsimd.affine_select(out=ident[:], in_=ident[:], compare_op=ALU.not_equal, fill=1.0, base=0,
                                        pattern=[[-1, P]], channel_multiplier=1).then_inc(ident_step, 1)
                pool.wait_ge(const_made, 2)
            pool_rstd(pool, 0)
            pool_rstd(pool, 1)
            if load:
                for k in range(EARLY):
                    full, hi, lo, _ = parts[k]
                    pool.wait_ge(whi_done, k + 1)
                    nc.gpsimd.tensor_tensor(lo, full, hi.bitcast(F32), ALU.subtract).then_inc(early_split, 1)
            for u in range(HEAD):
                pool_unit(pool, 0, u, 0)
            with pool.Fori(0, GROUPS // 2 - 1) as turn:
                pool_group(pool, 2 * turn, 0, False)
                pool_group(pool, 2 * turn + 1, 1, False)
            pool_group(pool, GROUPS - 2, 0, False)
            pool_group(pool, GROUPS - 1, 1, True)

        def dve_unit(dve, g, u):
            U = g * UNITS + u
            wait(dve, h0_ready, U + 1)
            wait(dve, gated_done, U + 1)
            if not (isinstance(U, int) and U < 4):
                wait(dve, hi_done, U - 3)
                wait(dve, lo_done, U - 3)
            nc.vector.scalar_tensor_tensor(out=act_sb[:, u % 4, :], in0=ps[:, H0[u % 2], :],
                                           scalar=bias0[:, u:u + 1], in1=gated[:, u % 2, :],
                                           op0=ALU.add, op1=ALU.mult).then_inc(act_done, 1)

        def dve_lo_part(dve, g, u):
            U = g * UNITS + u
            wait(dve, hi_done, U + 1)
            if not (isinstance(U, int) and U < 4):
                wait(dve, w2_done, U - 3)
            nc.vector.tensor_tensor(act_lo[:, u % 4, :], act_sb[:, u % 4, :],
                                    act_hi[:, u % 4, :].bitcast(F32), ALU.subtract).then_inc(lo_done, 1)

        def dve_stats(dve, g):
            gx = g % GROUPS
            if load and isinstance(g, int) and g < 3:
                dve.wait_ge(x_loaded[g], 16 if g < 2 else 16 * (GROUPS - 2))
                nc.vector.memset(spare[:, 0:1], 0.0)
            if not (isinstance(g, int) and g == 0):
                wait(dve, xn_ready, g)
            for t in range(TG):
                i = nc.vector.bn_stats(stats[:, t, :], xs[:, gx * TG + t, :])
            i.then_inc(bn_done, 1)
            dve.wait_ge(bn_done, g + 1)
            nc.vector.memset(spare[:, 0:1], 0.0)
            for t in range(TG):
                i = nc.vector.bn_aggr(mv[:, t, :], stats[:, t, :])
            i.then_inc(stats_ready, 1)

        def dve_norm(dve, g):
            wait(dve, rstd_step, 2 * g + 2)
            if not (isinstance(g, int) and g == 0):
                wait(dve, xT_ready, g)
            gx = g % GROUPS
            for t in range(TG):
                i = nc.vector.tensor_scalar(xn[:, t, :], xs[:, gx * TG + t, :], mv[:, t, 0:1],
                                            rstd[:, t:t + 1], ALU.subtract, ALU.mult)
            i.then_inc(xn_ready, 1)

        def dve_xsplit(dve, g, par):
            wait(dve, xf_ready, g + 1)
            if not (isinstance(g, int) and g < 2):
                wait(dve, h0_ready, (g - 1) * UNITS)
            nc.vector.tensor_copy(x_hi[:, par, :], ps[:, XT, :]).then_inc(xhi_done, 1)
            dve.wait_ge(xhi_done, g + 1)
            nc.vector.tensor_tensor(x_lo[:, par, :], ps[:, XT, :], x_hi[:, par, :].bitcast(F32),
                                    ALU.subtract).then_inc(xsplit_ready, 1)

        def dve_top(dve, g):
            wait(dve, logits_ready, g + 1)
            nc.vector.tensor_tensor(logits[:], ps[:, LG, 0:TG * E].rearrange("p (t e) -> p t e", e=E),
                                    gb[:].unsqueeze(1).broadcast_to([P, TG, E]), ALU.add).then_inc(logits_done, 1)
            dve.wait_ge(logits_done, g + 1)
            nc.vector.memset(spare[:, 1:2], 0.0)
            for t in range(TG):
                i = nc.vector.max(top[:, t, :], logits[:, t, :])
            i.then_inc(top_done, 1)
            dve.wait_ge(top_done, g + 1)
            if not (isinstance(g, int) and g == 0):
                wait(dve, tanh_ready, g)
            nc.vector.tensor_tensor(diff[:], top[:, :, 0], top[:, :, 1], ALU.subtract).then_inc(diff_ready, 1)
            for t in range(TG):
                i = nc.vector.max_index(top_i[:, t, :], top[:, t, :], logits[:, t, :])
            i.then_inc(index_done, 1)
            dve.wait_ge(index_done, g + 1)
            nc.vector.tensor_copy(top_f[:], top_i[:, :, 0:2]).then_inc(topf_done, 1)

        def dve_gates(dve, g):
            wait(dve, tanh_ready, g + 1)
            nc.vector.tensor_scalar(w12[:, 0, :], th[:], 0.25, 0.25, ALU.mult, ALU.add)
            nc.vector.tensor_scalar(w12[:, 1, :], th[:], -0.25, 0.25, ALU.mult, ALU.add).then_inc(w12_done, 1)
            dve.wait_ge(topf_done, g + 1)
            for r in range(2):
                i = nc.vector.tensor_tensor(pick[:, r], iota[:].unsqueeze(1).broadcast_to([P, TG, E]),
                                            top_f[:, :, r:r + 1].broadcast_to([P, TG, E]), ALU.is_equal)
            i.then_inc(match_done, 1)
            dve.wait_ge(w12_done, g + 1)
            dve.wait_ge(match_done, g + 1)
            for r in range(2):
                i = nc.vector.tensor_tensor(pick[:, r], pick[:, r],
                                            w12[:, r, :].unsqueeze(2).broadcast_to([P, TG, E]), ALU.mult)
            i.then_inc(pick_done, 1)
            dve.wait_ge(pick_done, g + 1)
            if not (isinstance(g, int) and g == 0):
                wait(dve, gT_ready, g)
            nc.vector.tensor_tensor(gpad[:, :, 0:E], pick[:, 0], pick[:, 1], ALU.add).then_inc(gates_ready, 1)

        def dve_gsplit(dve, g):
            wait(dve, gf_ready, g + 1)
            if not (isinstance(g, int) and g == 0):
                wait(dve, w2_done, (g - 1) * UNITS + 1)
            nc.vector.tensor_copy(g_hi[:], ps[:, GT, :]).then_inc(ghi_done, 1)
            dve.wait_ge(ghi_done, g + 1)
            nc.vector.tensor_tensor(g_lo[:], ps[:, GT, :], g_hi[:].bitcast(F32), ALU.subtract).then_inc(gsplit_ready, 1)

        def dve_close(dve, g):
            wait(dve, yT_ready, g + 1)
            tiles = xs[:, g * TG:(g + 1) * TG, :] if isinstance(g, int) else xs[:, bass.ts(g, TG), :]
            nc.vector.tensor_tensor(tiles, tiles, ps[:, GT, :].rearrange("p (t d) -> p t d", d=P),
                                    ALU.add).then_inc(x_updated, 1)

        def dve_split(dve, k):
            if k < len(parts):
                full, hi, lo, _ = parts[k]
                dve.wait_ge(whi_done, k + 1)
                nc.vector.tensor_tensor(lo, full, hi.bitcast(F32), ALU.subtract).then_inc(split_done, 1)

        def dve_group(dve, g, last):
            for v in range(HEAD, UNITS + HEAD):
                if v < UNITS:
                    dve_unit(dve, g, v)
                elif not last:
                    dve_unit(dve, g + 1, v - UNITS)
                if v - 1 < UNITS:
                    dve_lo_part(dve, g, v - 1)
                elif not last:
                    dve_lo_part(dve, g + 1, v - 1 - UNITS)
                if v == HEAD and not (isinstance(g, int) and g == 0):
                    dve_close(dve, g - 1)
                if load and isinstance(g, int) and g == 0 and v < UNITS:
                    dve_split(dve, v + EARLY - 1)
                if not last:
                    if v == 5:
                        dve_xsplit(dve, g + 1, (g + 1) % 2)
                    if v == 6:
                        dve_top(dve, g + 1)
                    if v == 8:
                        dve_gates(dve, g + 1)
                    if v == 12:
                        dve_gsplit(dve, g + 1)
                    if v == 13:
                        dve_stats(dve, g + 2)
                    if v == 16:
                        dve_norm(dve, g + 2)
            if last:
                dve_close(dve, g)

        @block.vector
        def _(dve):
            if load:
                nc.vector.memset(b2_f[:], 0.0).then_inc(b2_zero, 1)
                nc.vector.memset(neg_half[:], -0.5).then_inc(const_made, 1)
                nc.vector.memset(eps_sb[:], EPS).then_inc(const_made, 1)
            nc.vector.memset(gpad[:], 0.0).then_inc(gpad_zero, 1)
            dve_stats(dve, 0)
            dve_norm(dve, 0)
            dve_stats(dve, 1)
            dve_xsplit(dve, 0, 0)
            if load:
                dve.wait_ge(ident_step, 3)
                nc.vector.tensor_copy(identb[:], ident[:])
                nc.vector.tensor_copy(iota[:], iota_i[:])
                dve.wait_ge(router_loaded, 2 * 16)
            dve_top(dve, 0)
            dve.wait_ge(gpad_zero, 1)
            dve_gates(dve, 0)
            dve_gsplit(dve, 0)
            dve_norm(dve, 1)
            if load:
                dve.wait_ge(const_loaded, 2 * 16)
            for u in range(HEAD):
                dve_unit(dve, 0, u)
                if u:
                    dve_lo_part(dve, 0, u - 1)
                    if load:
                        dve_split(dve, EARLY + u - 1)
            dve_group(dve, 0, False)
            with dve.Fori(1, GROUPS - 1) as g:
                dve_group(dve, g, False)
            dve_group(dve, GROUPS - 1, True)

        def sp_gates(sp, g):
            wait(sp, gf_ready, g + 1)
            sp.dma_start(gate_dram[g], g_f[:]).then_inc(gates_out, 16)
            sp.wait_ge(gates_out, 16 * g + 16)
            wait(sp, gated_done, (g - 1) * UNITS)
            for part, es in enumerate((slice(0, FIRST), slice(FIRST, E))):
                sp.dma_start(gates_bc[:, g % 2, es, :],
                             gate_dram[g, es].partition_broadcast(P)).then_inc(gates_in[part], 16)

        def sp_store(sp, g):
            wait(sp, x_updated, g + 1)
            for j in range(T // S):
                b = g * (T // S) + j
                sp.dma_start(out_dram[:, b], xs[:, 2 * b:2 * b + 2, :]).then_inc(stored, 16)

        def sp_load(sp):
            sp.wait_ge(b2_zero, 1)
            for q in range(E // 2):
                cols = slice(q * 2 * HID, (q + 1) * 2 * HID)
                for w in (1, 0, 2):
                    sp.dma_start(stage[w][:, cols], dram[f"w{w}"][:, cols]).then_inc(parts[part_at[w, q] - 1][3][0], 16)
                    if (w, q) == (0, 0):
                        sp.dma_start(b2_f[0:E, :], dram["b2"]).then_inc(b2_part[3][0], 16)
                if q == 0:
                    sp.dma_start(xv(1), dram["x"][:, 2:4]).then_inc(x_loaded[1], 16)
            for g in range(2, GROUPS):
                sp.dma_start(xv(g), dram["x"][:, 2 * g:2 * g + 2]).then_inc(x_loaded[2], 16)
            sp.dma_start(bo_sb[:], dram["bo"].partition_broadcast(P)).then_inc(attn_loaded, 16)
            for dst, n in ((wqk_f[0:HALF, 0:HALF], "wk"), (wqk_f[HALF:P, 0:HALF], "wk"),
                           (wqk_f[0:HALF, HALF:P], "wq"), (wqk_f[HALF:P, HALF:P], "wq"),
                           (wv_f[0:HALF, :], "wv"), (wv_f[HALF:P, :], "wv"),
                           (wo_f[0:HALF, :], "wo"), (wo_f[HALF:P, :], "wo")):
                sp.dma_start(dst, dram[n]).then_inc(attn_loaded, 16)

        @block.sync
        def _(sp):
            if load:
                sp_load(sp)
            for g in range(GROUPS + 1):
                if g < GROUPS:
                    sp_gates(sp, g)
                if g and out_dram is not None:
                    sp_store(sp, g - 1)
            if out_dram is not None:
                sp.wait_ge(stored, 16 * NB)


def attention(nc, xs, ident, identb, wqk_hi, wqk_lo, wv_hi, wv_lo, wo_hi, wo_lo, bo_sb, eps_sb,
              neg_half, kq_dram, ps):
    NJ = 4
    HG = NH // NJ
    KP, KM = 24, 27
    SCALE = float(P // NH) ** -0.5
    UR = NH
    SBK, O, MISC_A, MISC_B = (3, 4), 5, 6, 7
    SA = (0, 1, 2) * 5 + (1,)
    with ExitStack() as c:
        def sb(n, shape, dt=F32):
            return c.enter_context(nc.sbuf_tensor(f"attn_{n}", shape, dt))

        def sem(n):
            return c.enter_context(nc.semaphore(f"attn_{n}"))

        qa = [sb(f"qa{i}", [P, NH, S], BF16) for i in range(4)]
        ka = [sb(f"ka{i}", [P, NH, S], BF16) for i in range(4)]
        va = [sb(f"va{i}", [P, 2, NH, 32]) for i in range(4)]
        ones_rows = sb("ones_rows", [3, S], BF16)
        pt = sb("pt", [P, 2, NJ, 2 * S])
        stats, mv = sb("stats", [P, 2, 6]), sb("mv", [P, 2, 2])
        vare, rstd = sb("vare", [P, 2]), sb("rstd", [P, 2])
        xn = sb("xn", [P, 2, 2, HALF])
        xT = sb("xT", [P, S], F32R)
        kqp = sb("kqp", [P, 3, S], BF16)
        rem = sb("rem", [P, S])
        nm = sb("nm", [P, 2, NH])
        nmr = sb("nmr", [P, 2, NH])
        mp = sb("mp", [P, 2, 8, NH], BF16)
        mT = sb("mT", [3 * NH, S], BF16)
        spare = sb("spare", [P, 1])
        oT = sb("oT", [P, 2 * S])
        rsum = sb("rsum", [P, 2, 2, NJ])
        otok = sb("otok", [P, 2, HALF])
        osp = sb("osp", [P, 2, 2, HALF])
        oTs = sb("oTs", [P, S], F32R)

        mp_zero, zeros_out, slot0_zeroed = sem("mp_zero"), sem("zeros_out"), sem("slot0_zeroed")
        zeroed, ones_made, ones_in, v_init = sem("zeroed"), sem("ones_made"), sem("ones_in"), sem("v_init")
        bn_done, stats_ready, rstd_step, xn_ready = sem("bn_done"), sem("stats_ready"), sem("rstd_step"), sem("xn_ready")
        xT_ready, xhi_done, xT_split = sem("xT_ready"), sem("xhi_done"), sem("xT_split")
        proj_ready, p0_done, v_copied = sem("proj_ready"), sem("p0_done"), sem("v_copied")
        rem_done, p1_done, pieces_ready = sem("rem_done"), sem("p1_done"), sem("pieces_ready")
        pieces_out, ops_in = sem("pieces_out"), sem("ops_in")
        rows_ready, max_done = sem("rows_ready"), sem("max_done")
        m0_done, mr_done, m1_done, m_ready = sem("m0_done"), sem("mr_done"), sem("m1_done"), sem("m_ready")
        mT_ready, mT_copied, m_in = sem("mT_ready"), sem("mT_copied"), sem("m_in")
        cols_ready, exp_done, pv_done = sem("cols_ready"), sem("exp_done"), sem("pv_done")
        oT_copied, otok_ready, recip_done, norm_done = sem("oT_copied"), sem("otok_ready"), sem("recip_done"), sem("norm_done")
        ohi_done, osp_ready, oTs_ready, oTs_copied = sem("ohi_done"), sem("osp_ready"), sem("oTs_ready"), sem("oTs_copied")
        y_ready, x_updated, bias_added = sem("y_ready"), sem("x_updated"), sem("bias_added")
        block = c.enter_context(nc.Block())

        def first(v, n=1):
            return isinstance(v, int) and v < n

        def valid(b):
            return not isinstance(b, int) or 0 <= b < NB

        def run_steps(eng, step):
            for s in range(-1, 4):
                step(eng, s, s % 4)
            with eng.Fori(1, 3) as turn:
                for i in range(4):
                    step(eng, turn * 4 + i, i)
            for s in range(12, NB + 3):
                step(eng, s, s % 4)

        def misc_uses(s, bank):
            if bank == MISC_A:
                uses = [("project", s + 1, rem_done, s + 2), ("xT", s + 2, xT_split, s + 3),
                        ("otok0", s - 2, norm_done, 2 * (s - 2) + 1)]
            else:
                uses = [("mT", s - 1, mT_copied, s), ("otok1", s - 3, norm_done, 2 * (s - 3) + 2),
                        ("oTs", s - 3, oTs_copied, s - 2), ("out", s - 3, x_updated, s - 2)]
            return [u for u in uses if valid(u[1])]

        def misc_free(eng, s, bank, name):
            before = misc_uses(s - 1, bank)
            uses = before + misc_uses(s, bank)
            at = len(before) + [u[0] for u in misc_uses(s, bank)].index(name)
            if at:
                _, _, semaphore, value = uses[at - 1]
                wait(eng, semaphore, value)

        def pe_cols(pe, b, sl, h):
            n = NH * b + h
            if h == 0:
                wait(pe, m_in, 48 * (b + 1))
            if not first(n, 2):
                wait(pe, exp_done, n - 1)
            for kc in range(2):
                mm = pe.matmul(ps[:, SBK[h % 2], kc * S:(kc + 1) * S], ka[sl][:, h, kc * P:(kc + 1) * P],
                               qa[sl][:, h, :], start=True, stop=True)
            mm.then_inc(cols_ready, 1)

        def pe_rows(pe, b, sl, k):
            pair, qc = divmod(k, 2)
            if k == 0:
                wait(pe, ops_in, 16 * 6 * (b + 1))
                if first(b, 4):
                    wait(pe, ones_in, 16 * (b + 1))
            ago = (SA[:k][::-1] + SA[::-1]).index(SA[k]) + 1
            n = UR * b + k
            if not first(n, ago):
                wait(pe, max_done, n - ago + 1)
            for j in range(2):
                h = 2 * pair + j
                mm = pe.matmul(ps[:, SA[k], j * S:(j + 1) * S],
                               qa[sl][:, h, qc * P:(qc + 1) * P], ka[sl][:, h, :], start=True, stop=True)
            mm.then_inc(rows_ready, 1)

        def pe_values(pe, b, sl, g):
            if g == 0:
                wait(pe, v_copied, b + 1)
            wait(pe, exp_done, NH * b + NJ * (g + 1))
            if g % 2 == 0 and not first(HG * b + g, 2):
                wait(pe, oT_copied, 2 * b + g // 2)
            for kc in range(2):
                for j in range(NJ):
                    mm = pe.matmul(ps[32 * j:32 * j + 32, O, (g % 2) * S:(g % 2 + 1) * S],
                                   va[sl][:, kc, NJ * g + j, :], pt[:, g % 2, j, kc * S:(kc + 1) * S],
                                   start=(kc == 0), stop=(kc == 1), tile_position=(0, 32 * j))
            mm.then_inc(pv_done, 1)

        def pe_xT(pe, b):
            wait(pe, xn_ready, b + 1)
            misc_free(pe, b - 2, MISC_A, "xT")
            for j in range(2):
                mm = pe.transpose(ps[:, MISC_A, j * P:(j + 1) * P], xn[:, j].rearrange("p a d -> p (a d)"), ident[:])
            mm.then_inc(xT_ready, 1)

        def pe_mT(pe, b):
            wait(pe, m_ready, b + 1)
            misc_free(pe, b + 1, MISC_B, "mT")
            for qc in range(2):
                mm = pe.transpose(ps[:, MISC_B, qc * HALF:(qc + 1) * HALF].bitcast(BF16),
                                  mp[:, qc].rearrange("p a h -> p (a h)"), identb[:])
            mm.then_inc(mT_ready, 1)

        def pe_project(pe, b):
            wait(pe, xT_split, b + 1)
            misc_free(pe, b - 1, MISC_A, "project")
            pe.matmul(ps[:, MISC_A, 0:S], wqk_hi[:], xT[:], start=True, stop=False, skip_group_check=True)
            pe.matmul(ps[:, MISC_A, 0:S], wqk_lo[:], xT[:], start=False, stop=True, skip_group_check=True)
            for j in range(2):
                o = ps[:, MISC_A, S + j * HALF:S + (j + 1) * HALF]
                pe.matmul(o, xT[:, j * P:(j + 1) * P], wv_hi[:], start=False, stop=False, skip_group_check=True)
                mm = pe.matmul(o, xT[:, j * P:(j + 1) * P], wv_lo[:], start=False, stop=True, skip_group_check=True)
            mm.then_inc(proj_ready, 1)

        MISC_OTOK = (MISC_A, MISC_B)

        def pe_otok(pe, b, pair):
            wait(pe, oT_copied, 2 * b + pair + 1)
            misc_free(pe, b + 3 if pair else b + 2, MISC_OTOK[pair], f"otok{pair}")
            for g in range(2):
                for qc in range(2):
                    mm = pe.transpose(ps[:, MISC_OTOK[pair], (2 * qc + g) * P:(2 * qc + g + 1) * P],
                                      oT[:, g * S + qc * P:g * S + (qc + 1) * P], ident[:])
            mm.then_inc(otok_ready, 1)

        def pe_oTs(pe, b):
            wait(pe, osp_ready, b + 1)
            misc_free(pe, b + 3, MISC_B, "oTs")
            for qc in range(2):
                mm = pe.transpose(ps[:, MISC_B, qc * P:(qc + 1) * P], osp[:, qc].rearrange("p a d -> p (a d)"), ident[:])
            mm.then_inc(oTs_ready, 1)

        def pe_out(pe, b):
            wait(pe, oTs_copied, b + 1)
            misc_free(pe, b + 3, MISC_B, "out")
            for qc in range(2):
                o = ps[:, MISC_B, qc * P:(qc + 1) * P]
                pe.matmul(o, oTs[:, qc * P:(qc + 1) * P], wo_hi[:], start=True, stop=False)
                mm = pe.matmul(o, oTs[:, qc * P:(qc + 1) * P], wo_lo[:], start=False, stop=True)
            mm.then_inc(y_ready, 1)

        def pe_step(pe, s, sl):
            for k in range(UR):
                if valid(s - 2):
                    pe_cols(pe, s - 2, (sl - 2) % 4, k)
                if k == 2 and valid(s + 1):
                    pe_project(pe, s + 1)
                if k == 2 and valid(s - 1):
                    pe_mT(pe, s - 1)
                if k == 6 and valid(s - 3):
                    pe_otok(pe, s - 3, 1)
                if k == 8 and valid(s + 2):
                    pe_xT(pe, s + 2)
                if k == 10 and valid(s - 3):
                    pe_oTs(pe, s - 3)
                if k == 12 and valid(s - 3):
                    pe_out(pe, s - 3)
                if k == 11 and valid(s - 2):
                    pe_otok(pe, s - 2, 0)
                if valid(s):
                    pe_rows(pe, s, sl, k)
                if k == 1 and valid(s - 3):
                    pe_values(pe, s - 3, (sl - 3) % 4, 3)
                if k in (5, 9, 13) and valid(s - 2):
                    pe_values(pe, s - 2, (sl - 2) % 4, (k - 5) // 4)

        @block.tensor
        def _(pe):
            pe_xT(pe, 0)
            run_steps(pe, pe_step)

        def act_exp(act, b, h):
            g, j = divmod(h, NJ)
            if j == 0 and not first(HG * b + g, 2):
                wait(act, pv_done, HG * b + g - 1)
            wait(act, cols_ready, NH * b + h + 1)
            nc.scalar.activation(pt[:, g % 2, j, :], ps[:, SBK[h % 2], :], ACT.Exp, scale=SCALE).then_inc(exp_done, 1)

        def act_xhi(act, b):
            wait(act, xT_ready, b + 1)
            if not first(b):
                wait(act, proj_ready, b)
            nc.scalar.activation(xT[:], ps[:, MISC_A, 0:S], ACT.Copy).then_inc(xhi_done, 1)

        def act_mT(act, b):
            wait(act, mT_ready, b + 1)
            if not first(b):
                wait(act, m_in, 48 * b)
            nc.scalar.activation(mT[:], ps[0:3 * NH, MISC_B, 0:P].bitcast(BF16), ACT.Copy).then_inc(mT_copied, 1)

        def act_project(act, b, sl):
            wait(act, proj_ready, b + 1)
            if not first(b):
                wait(act, pieces_out, 16 * b)
            nc.scalar.activation(kqp[:, 0, :], ps[:, MISC_A, 0:S], ACT.Copy).then_inc(p0_done, 1)
            if not first(b, 4):
                wait(act, pv_done, HG * (b - 3))
            else:
                wait(act, v_init, 2 * b + 2)
            nc.scalar.activation(va[sl][:, :, :, 0:DH],
                                 ps[:, MISC_A, S:S + 2 * HALF].rearrange("p (c h d) -> p c h d", c=2, d=DH),
                                 ACT.Copy).then_inc(v_copied, 1)

        def act_oT(act, b, pair):
            wait(act, pv_done, HG * b + 2 * pair + 2)
            if not first(2 * b + pair):
                wait(act, otok_ready, 2 * b + pair)
            nc.scalar.activation(oT[:], ps[:, O, :], ACT.Copy).then_inc(oT_copied, 1)

        def act_oTs(act, b):
            wait(act, oTs_ready, b + 1)
            if not first(b):
                wait(act, y_ready, b)
            nc.scalar.activation(oTs[:], ps[:, MISC_B, 0:S], ACT.Copy).then_inc(oTs_copied, 1)

        def act_piece1(act, b):
            wait(act, rem_done, b + 1)
            nc.scalar.activation(kqp[:, 1, :], rem[:], ACT.Copy).then_inc(p1_done, 1)

        def act_step(act, s, sl):
            for k in range(UR):
                if k == 2 and valid(s - 3):
                    act_oT(act, s - 3, 1)
                if k == 10 and valid(s - 2):
                    act_oT(act, s - 2, 0)
                if valid(s - 2):
                    act_exp(act, s - 2, k)
                if k == 2 and valid(s + 1):
                    act_project(act, s + 1, (sl + 1) % 4)
                if k == 3 and valid(s - 1):
                    act_mT(act, s - 1)
                if k == 5 and valid(s + 1):
                    act_piece1(act, s + 1)
                if k == 8 and valid(s + 2):
                    act_xhi(act, s + 2)
                if k == 10 and valid(s - 3):
                    act_oTs(act, s - 3)

        @block.scalar
        def _(act):
            act_xhi(act, 0)
            run_steps(act, act_step)

        def pool_rstd(pool, b):
            wait(pool, stats_ready, b + 1)
            nc.gpsimd.tensor_tensor(vare[:], mv[:, :, 1], eps_sb[:, 0:2], ALU.add).then_inc(rstd_step, 1)
            pool.wait_ge(rstd_step, 2 * b + 1)
            nc.gpsimd.tensor_tensor(rstd[:], vare[:], neg_half[:, 0:2], ALU.pow).then_inc(rstd_step, 1)

        def tiles(b):
            return xs[:, 2 * b:2 * b + 2, :] if isinstance(b, int) else xs[:, bass.ts(b, 2), :]

        def pool_bias(pool, b):
            wait(pool, xn_ready, b + 1)
            nc.gpsimd.tensor_tensor(tiles(b), tiles(b), bo_sb[:].unsqueeze(1).broadcast_to([P, 2, P]),
                                    ALU.add).then_inc(bias_added, 1)

        def pool_olow(pool, b):
            wait(pool, ohi_done, b + 1)
            if not first(b):
                wait(pool, oTs_ready, b)
            nc.gpsimd.tensor_tensor(osp[:, :, 1, :], otok[:], osp[:, :, 0, :], ALU.subtract).then_inc(osp_ready, 1)

        def pool_piece2(pool, b):
            wait(pool, p1_done, b + 1)
            nc.gpsimd.tensor_tensor(kqp[:, 2, :], rem[:], kqp[:, 1, :], ALU.subtract).then_inc(pieces_ready, 1)

        def pool_values_init(pool, i):
            pool.memset(va[i][:], 0.0).then_inc(v_init, 1)
            pool.wait_ge(v_init, 2 * i + 1)
            pool.memset(va[i][:, :, :, DH:DH + 1], 1.0).then_inc(v_init, 1)

        def pool_step(pool, s, sl):
            if valid(s + 2):
                pool_rstd(pool, s + 2)
            if valid(s + 1):
                pool_piece2(pool, s + 1)
            if first(s, 2):
                pool.memset(qa[s + 2][:].bitcast(U32), 0).then_inc(zeroed, 1)
                pool.memset(ka[s + 2][:].bitcast(U32), 0).then_inc(zeroed, 1)
                pool_values_init(pool, s + 2)
            if valid(s - 3):
                pool_olow(pool, s - 3)
            if valid(s + 2):
                pool_bias(pool, s + 2)

        @block.gpsimd
        def _(pool):
            pool_rstd(pool, 0)
            pool.memset(ones_rows[:], 1.0).then_inc(ones_made, 1)
            pool_values_init(pool, 0)
            pool_bias(pool, 0)
            run_steps(pool, pool_step)

        def dve_stats(dve, b):
            if not first(b):
                wait(dve, xn_ready, b)
            for j in range(2):
                i = nc.vector.bn_stats(stats[:, j, :], xs[:, 2 * b + j, :])
            i.then_inc(bn_done, 1)
            wait(dve, bn_done, b + 1)
            nc.vector.memset(spare[:], 0.0)
            for j in range(2):
                i = nc.vector.bn_aggr(mv[:, j, :], stats[:, j, :])
            i.then_inc(stats_ready, 1)

        def dve_norm(dve, b):
            wait(dve, rstd_step, 2 * b + 2)
            if not first(b):
                wait(dve, xT_ready, b)
            for j in range(2):
                i = nc.vector.tensor_scalar(xn[:, j], xs[:, 2 * b + j, 0:HALF].unsqueeze(1).broadcast_to([P, 2, HALF]),
                                            mv[:, j, 0:1], rstd[:, j:j + 1], ALU.subtract, ALU.mult)
            i.then_inc(xn_ready, 1)

        def dve_xlo(dve, b):
            wait(dve, xhi_done, b + 1)
            nc.vector.tensor_tensor(xT[HALF:P, :], ps[HALF:P, MISC_A, 0:S], xT[HALF:P, :].bitcast(F32),
                                    ALU.subtract).then_inc(xT_split, 1)

        def dve_rem(dve, b):
            wait(dve, v_copied, b + 1)
            if not first(b):
                wait(dve, pieces_ready, b)
            nc.vector.tensor_tensor(rem[:], ps[:, MISC_A, 0:S], kqp[:, 0, :], ALU.subtract).then_inc(rem_done, 1)

        def dve_max(dve, b, k):
            pair, qc = divmod(k, 2)
            wait(dve, rows_ready, UR * b + k + 1)
            if k == 0 and first(b):
                dve.wait_ge(mp_zero, 1)
            elif k == 0:
                wait(dve, m_ready, b)
            nc.vector.tensor_reduce(nm[:, qc, 2 * pair:2 * pair + 2],
                                    ps[:, SA[k], :].rearrange("p (j t) -> p j t", t=S),
                                    AX.X, ALU.max, negate=True).then_inc(max_done, 1)

        def dve_m(dve, b):
            wait(dve, max_done, UR * (b + 1))
            if not first(b):
                wait(dve, mT_ready, b)
            nc.vector.tensor_copy(mp[:, :, 0, :], nm[:]).then_inc(m0_done, 1)
            wait(dve, m0_done, b + 1)
            nc.vector.tensor_tensor(nmr[:], nm[:], mp[:, :, 0, :], ALU.subtract).then_inc(mr_done, 1)
            wait(dve, mr_done, b + 1)
            nc.vector.tensor_copy(mp[:, :, 1, :], nmr[:]).then_inc(m1_done, 1)
            wait(dve, m1_done, b + 1)
            nc.vector.tensor_tensor(mp[:, :, 2, :], nmr[:], mp[:, :, 1, :], ALU.subtract).then_inc(m_ready, 1)

        def dve_otok(dve, b, pair):
            n = 2 * b + pair
            wait(dve, otok_ready, n + 1)
            o = ps[:, MISC_OTOK[pair], :].rearrange("p (c h k) -> p c h k", c=2, k=32)
            if not first(n):
                wait(dve, norm_done, n)
            nc.vector.reciprocal(rsum[:].rearrange("p c g j -> p c (g j)"), o[:, :, :, DH]).then_inc(recip_done, 1)
            wait(dve, recip_done, n + 1)
            if pair == 0 and not first(b):
                wait(dve, osp_ready, b)
            nc.vector.tensor_tensor(
                otok[:, :, pair * 32:pair * 32 + 32].rearrange("p c (h d) -> p c h d", d=DH), o[:, :, :, 0:DH],
                rsum[:].rearrange("p c g j -> p c (g j)").unsqueeze(3).broadcast_to([P, 2, 2 * NJ, DH]),
                ALU.mult).then_inc(norm_done, 1)

        def dve_ohi(dve, b):
            wait(dve, norm_done, 2 * b + 2)
            if not first(b):
                wait(dve, oTs_ready, b)
            nc.vector.tensor_copy(osp[:, :, 0, :].bitcast(F32R), otok[:]).then_inc(ohi_done, 1)

        def dve_residual(dve, b):
            wait(dve, y_ready, b + 1)
            wait(dve, bias_added, b + 1)
            t = tiles(b)
            nc.vector.tensor_tensor(t, t, ps[:, MISC_B, 0:S].rearrange("p (t d) -> p t d", d=P), ALU.add).then_inc(x_updated, 1)

        def dve_step(dve, s, sl):
            for k in range(UR):
                if k == 3 and valid(s + 1):
                    dve_rem(dve, s + 1)
                if valid(s):
                    dve_max(dve, s, k)
                if k == 1 and valid(s + 2):
                    dve_stats(dve, s + 2)
                if k == 6 and valid(s - 3):
                    dve_otok(dve, s - 3, 1)
                    dve_ohi(dve, s - 3)
                if k == 5 and valid(s + 2):
                    dve_norm(dve, s + 2)
                if k == 8 and valid(s + 2):
                    dve_xlo(dve, s + 2)
                if k == 12 and valid(s - 3):
                    dve_residual(dve, s - 3)
                if k == 10 and valid(s - 2):
                    dve_otok(dve, s - 2, 0)
                if k == UR - 1 and valid(s):
                    dve_m(dve, s)

        @block.vector
        def _(dve):
            dve.memset(mp[:], 0.0).then_inc(mp_zero, 1)
            dve_stats(dve, 0)
            dve.memset(qa[0][:].bitcast(U32), 0).then_inc(slot0_zeroed, 1)
            dve_norm(dve, 0)
            dve_xlo(dve, 0)
            dve.memset(ka[0][:].bitcast(U32), 0).then_inc(slot0_zeroed, 1)
            run_steps(dve, dve_step)

        def sp_constant_rows(sp, i):
            if i == 0:
                sp.wait_ge(slot0_zeroed, 2)
            else:
                sp.wait_ge(zeroed, 2 * i)
            sp.dma_start(ka[i][KP:KM], ones_rows[:].unsqueeze(1).broadcast_to([3, NH, S])).then_inc(ones_in, 16)

        def sp_pieces(sp, b):
            if b == 0:
                sp_constant_rows(sp, 0)
            wait(sp, pieces_ready, b + 1)
            sp.dma_start(kq_dram[b, 0:3].rearrange("a i c t -> (i c) a t"), kqp[:]).then_inc(pieces_out, 16)

        def sp_operands(sp, b, sl):
            if first(b, 4):
                if b:
                    sp_constant_rows(sp, b)
            else:
                wait(sp, cols_ready, NH * (b - 3))
            wait(sp, pieces_out, 16 * (b + 1))
            kq = kq_dram[b].rearrange("a i (d h) t -> a i d (h t)", d=DH)
            kv, qv = (t[sl][:].rearrange("p h t -> p (h t)") for t in (ka, qa))
            r = 0
            for n in (3, 2, 1):
                sp.dma_start(kv[r:r + n * DH, :], kq[0:n, 0]).then_inc(ops_in, 16)
                r += n * DH
            r = 0
            for piece, n in enumerate((3, 2)):
                sp.dma_start(qv[r:r + n * DH, :], kq[piece, 1].unsqueeze(0).broadcast_to([n, DH, NH * S])).then_inc(ops_in, 16)
                r += n * DH
            rows = kq_dram[b].rearrange("a i (d h) t -> (a i d) (h t)", d=DH)
            sp.dma_start(qv[r:KM, :], rows[5 * DH:5 * DH + KM - r]).then_inc(ops_in, 16)

        def sp_max(sp, b, sl):
            wait(sp, mT_copied, b + 1)
            for i in range(3):
                sp.dma_start(qa[sl][KP + i:KP + i + 1], mT[NH * i:NH * i + NH, :]).then_inc(m_in, 16)

        def sp_step(sp, s, sl):
            if valid(s - 1):
                sp_max(sp, s - 1, (sl - 1) % 4)
            if valid(s + 1):
                sp_pieces(sp, s + 1)
                sp_operands(sp, s + 1, (sl + 1) % 4)

        @block.sync
        def _(sp):
            sp.wait_ge(slot0_zeroed, 1)
            zero_rows = kq_dram[:, 3, 0].rearrange("b (d h) t -> b d (h t)", d=DH)[:, 0:KM - KP]
            sp.dma_start(zero_rows.rearrange("b d n -> d b n"), qa[0][0:(KM - KP)].rearrange("p h t -> p (h t)").unsqueeze(1).broadcast_to([KM - KP, NB, NH * S])).then_inc(zeros_out, 16)
            sp.wait_ge(zeros_out, 16)
            sp.wait_ge(ones_made, 1)
            for s in range(-1, NB + 3):
                sp_step(sp, s, s % 4)


def kernel(L0_attn_x, L0_attn_Wq, L0_attn_Wk, L0_attn_Wv, L0_attn_Wo, L0_attn_bo, L0_ffn_gate_w,
           L0_ffn_gate_b, L0_ffn_w0, L0_ffn_b0, L0_ffn_w1, L0_ffn_b1, L0_ffn_w2, L0_ffn_b2):
    import numpy as np
    import concourse.bacc as bacc
    from concourse import mybir as mb
    from concourse.bass_utils import run_bass_kernel_spmd

    def np32(a):
        return np.asarray(a)

    def head_minor(w):
        return np32(w).reshape(NH, DH, HALF).transpose(1, 0, 2).reshape(HALF, HALF)

    arrays = {
        "x": np32(L0_attn_x),
        "gate_wT": np32(L0_ffn_gate_w).T,
        "gate_b": np32(L0_ffn_gate_b).reshape(E),
        "w0T": np32(L0_ffn_w0).transpose(2, 0, 1).reshape(P, E * HID),
        "b0T": np32(L0_ffn_b0).reshape(UNITS, P).T,
        "w1T": np32(L0_ffn_w1).transpose(2, 0, 1).reshape(P, E * HID),
        "b1T": np32(L0_ffn_b1).reshape(UNITS, P).T,
        "w2T": np32(L0_ffn_w2).reshape(E, P, CH, P).transpose(3, 0, 2, 1).reshape(P, E * HID),
        "b2": np32(L0_ffn_b2),
        "wqT": head_minor(L0_attn_Wq).T,
        "wkT": head_minor(L0_attn_Wk).T,
        "wvT": np32(L0_attn_Wv).T,
        "woT": np32(L0_attn_Wo).T,
        "bo": np32(L0_attn_bo),
    }
    arrays = {k: np.ascontiguousarray(v) for k, v in arrays.items()}
    nc = bacc.Bacc("TRN2", target_bir_lowering=False, num_devices=1)
    aps = {k: nc.dram_tensor(k, v.shape, F32, kind="ExternalInput").ap() for k, v in arrays.items()}
    out = nc.dram_tensor("out", (NB, S, P), F32, kind="ExternalOutput").ap()
    macaron(nc, **aps, out=out)
    r = run_bass_kernel_spmd(nc, [arrays], core_ids=[0])
    return r.results[0]["out"]
```

```python
from contextlib import ExitStack

import concourse.bass as bass
from concourse import mybir

ALU = mybir.AluOpType
ACT = mybir.ActivationFunctionType
AX = mybir.AxisListType
F32 = mybir.dt.float32
F32R = mybir.dt.float32r
BF16 = mybir.dt.bfloat16
U32 = mybir.dt.uint32

P = 128
NB, S = 16, 256
TILES = NB * S // P
E, HID = 8, 256
CH = HID // P
T = 512
TG = T // P
GROUPS = NB * S // T
UNITS = E * CH
NH, DH, HALF = 16, 4, 64
EPS = 1e-5
FIRST = 2
LAG = 3
LOGITS, GATES = 7, 11
STATS, NORM = 14, 16
HEAD = LAG + 1


def wait(eng, sem, value):
    if isinstance(value, int) and value <= 0:
        return
    eng.wait_ge(sem, value)


def macaron(nc, x, gate_wT, gate_b, w0T, b0T, w1T, b1T, w2T, b2, wqT, wkT, wvT, woT, bo, out):
    x_dram = x.rearrange("b (p j) d -> p b j d", j=2)
    out_dram = out.rearrange("b (p j) d -> p b j d", j=2)
    kq_dram = nc.dram_tensor("kq_pieces", [NB, 4, 2, HALF, S], BF16)
    gate_dram = nc.dram_tensor("gates", [2, GROUPS, E, T], F32)

    with ExitStack() as ctx:
        def sb(name, shape, dt=F32, c=ctx):
            return c.enter_context(nc.sbuf_tensor(name, shape, dt))

        xs = sb("x_tokens", [P, TILES, P])
        ident = sb("ident", [P, P])
        identb = sb("identb", [P, P], BF16)
        w_hi = [sb(f"w{i}_hi", [P, E * HID], F32R) for i in range(3)]
        w_lo = [sb(f"w{i}_lo", [P, E * HID], F32R) for i in range(3)]
        b2_st = sb("b2_stacked", [P, P], F32R)
        wqk_hi, wqk_lo = sb("wqk_hi", [P, P], F32R), sb("wqk_lo", [P, P], F32R)
        wv_hi, wv_lo = sb("wv_hi", [P, HALF], F32R), sb("wv_lo", [P, HALF], F32R)
        wo_hi, wo_lo = sb("wo_hi", [P, P], F32R), sb("wo_lo", [P, P], F32R)
        gw_hl, gw_h0 = sb("gate_w_hi_lo", [P, 2 * E], F32R), sb("gate_w_hi_0", [P, 2 * E], F32R)
        gb = sb("gate_b_sb", [P, E])
        bias0 = sb("bias0", [P, UNITS])
        bias1 = sb("bias1", [P, UNITS])
        bo_sb = sb("bo_sb", [P, P])
        iota = sb("iota", [P, E])
        neg_half = sb("neg_half", [P, TG])
        eps_sb = sb("eps_sb", [P, TG])
        ps = ctx.enter_context(nc.psum_tensor("ps", [P, 8, T], F32))

        weights = (w_hi, w_lo, b2_st, gw_hl, gw_h0, gb, bias0, bias1, iota, neg_half, eps_sb)
        dram = dict(w0=w0T, w1=w1T, w2=w2T, b2=b2, wq=wqT, wk=wkT, wv=wvT, wo=woT, bo=bo,
                    gate_w=gate_wT, gate_b=gate_b, b0=b0T, b1=b1T, x=x_dram)
        attn_weights = (wqk_hi, wqk_lo, wv_hi, wv_lo, wo_hi, wo_lo, bo_sb, identb)
        stages = sb("stages", [P, 3 * E * HID])
        stage = [stages[:, i * E * HID:(i + 1) * E * HID] for i in range(3)]
        attn = attention(nc, ctx, xs, ident, identb, wqk_hi, wqk_lo, wv_hi, wv_lo, wo_hi, wo_lo, bo_sb,
                         eps_sb, neg_half, kq_dram, ps, stage)
        with ExitStack() as c:
            ffn(nc, c, "ffn1", (0, 1, 2, 3, 4, 5, 6, 7), xs, ident, weights, gate_dram[0], ps, None,
                (dram, attn_weights, stage), attn, None)["run"]()
        ffn2 = ffn(nc, ctx, "ffn2", (3, 4, 5, 6, 7, 0, 1, 2), xs, ident, weights, gate_dram[1], ps, out_dram,
                   None, None, stages)
        attn["run"](ffn2)
        ffn2["run"]()


def ffn(nc, c, name, banks, xs, ident, weights, gate_dram, ps, out_dram, load, attn, spare_memory):
    w_hi, w_lo, b2_st, gw_hl, gw_h0, gb, bias0, bias1, iota, neg_half, eps_sb = weights
    H1, H0, Y, XT, LG, GT = banks[0:2], banks[2:4], *banks[4:]

    def sb(n, shape, dt=F32):
        return c.enter_context(nc.sbuf_tensor(f"{name}_{n}", shape, dt))

    def sem(n):
        return c.enter_context(nc.semaphore(f"{name}_{n}"))

    stats, mv = sb("stats", [P, TG, 6]), sb("mv", [P, TG, 2])
    vare, rstd = sb("vare", [P, TG]), sb("rstd", [P, TG])
    logits, top = sb("logits", [P, TG, E]), sb("top", [P, TG, E])
    top_i, top_f = sb("top_i", [P, TG, E], U32), sb("top_f", [P, TG, 2])
    diff, th, w12 = sb("diff", [P, TG]), sb("th", [P, TG]), sb("w12", [P, 2, TG])
    pick = sb("pick", [P, 2, TG, E])
    if spare_memory:
        def mem(i, n):
            return spare_memory[:, i * T:(i + n) * T]

        gates_bc = [mem(0, E).rearrange("p (e t) -> p e t", t=T)]
        xn, gpad = (mem(E + i, 1).rearrange("p (t d) -> p t d", d=P) for i in range(2))
        g_f = spare_memory[0:E, (E + 2) * T:(E + 3) * T]
    else:
        gates_bc = [sb("gates_bc0", [P, E, T])]
        xn, gpad = sb("xn", [P, TG, P])[:], sb("gpad", [P, TG, P])[:]
        g_f = sb("g_f", [E, T])[:]
    g_st = sb("g_stacked", [P, T], F32R)
    pre = sb("pre", [P, TG, E])
    x_hi, x_lo = sb("x_hi", [P, 2, T], F32R), sb("x_lo", [P, 2, T], F32R)
    silu = gated = act_sb = act_hi = act_lo = y_sb = None
    spare = sb("spare", [P, 2])
    if load:
        gw = sb("gate_w", [P, E])
        b2_f, wqk_f, wv_f, wo_f = sb("b2_f", [P, P]), sb("wqk_f", [P, P]), sb("wv_f", [P, HALF]), sb("wo_f", [P, P])
        iota_i = sb("iota_i", [P, E], mybir.dt.int32)
        dram, (wqk_hi, wqk_lo, wv_hi, wv_lo, wo_hi, wo_lo, bo_sb, identb), staged = load
        b2_part = (b2_f[:], b2_st[:], b2_st[:], (sem("b2_loaded"), 3), slice(64, 96))
        parts, part_at = [], {}
        for q in range(E // 2):
            cols = slice(q * 2 * HID, (q + 1) * 2 * HID)
            for w in (1, 0, 2):
                if (w, q) == (2, 0):
                    parts.append(b2_part)
                parts.append((staged[w][:, cols], w_hi[w][:, cols], w_lo[w][:, cols], (sem(f"w{w}_{q}_loaded"), 1), slice(0, P)))
                part_at[w, q] = len(parts)
        attn_loaded = sem("attn_weights_loaded")
        for f, h, l in ((wqk_f, wqk_hi, wqk_lo), (wv_f, wv_hi, wv_lo), (wo_f, wo_hi, wo_lo)):
            parts.append((f[:], h[:], l[:], (attn_loaded, 9), slice(0, P)))
        x_loaded = [sem("x0_loaded"), sem("x1_loaded"), sem("x_rest_loaded")]
        router_loaded, router_hi, router_split = sem("router_loaded"), sem("router_hi"), sem("router_split")
        const_loaded, const_made, whi_done = sem("const_loaded"), sem("const_made"), sem("whi_done")
        early_split, split_done = sem("early_split"), sem("split_done")
        b2_zero, ident_step = sem("b2_zero"), sem("ident_step")
    EARLY, NEXT = 4, 7

    stats_ready, rstd_step, xn_ready = sem("stats_ready"), sem("rstd_step"), sem("xn_ready")
    xT_ready, xsplit_ready, pre_done = sem("xT_ready"), sem("xsplit_ready"), sem("pre_done")
    logits_ready, diff_ready, tanh_ready = sem("logits_ready"), sem("diff_ready"), sem("tanh_ready")
    gates_ready, gT_ready, gf_ready = sem("gates_ready"), sem("gT_ready"), sem("gf_ready")
    gsplit_ready, gates_out, gates_in = sem("gsplit_ready"), sem("gates_out"), (sem("gates_in_first"), sem("gates_in_rest"))
    h1_ready, h0_ready, silu_done = sem("h1_ready"), sem("h0_ready"), sem("silu_done")
    gated_done, act_done, hi_done, lo_done = sem("gated_done"), sem("act_done"), sem("hi_done"), sem("lo_done")
    w2_done = sem("w2_done")
    y_ready, y_copied, yT_ready = sem("y_ready"), sem("y_copied"), sem("yT_ready")
    x_updated, stored = sem("x_updated"), sem("stored")
    bn_done, xhi_done, logits_done, top_done = sem("bn_done"), sem("xhi_done"), sem("logits_done"), sem("top_done")
    index_done, topf_done, w12_done = sem("index_done"), sem("topf_done"), sem("w12_done")
    match_done, pick_done, ghi_done, gpad_zero = sem("match_done"), sem("pick_done"), sem("ghi_done"), sem("gpad_zero")

    def split_upto(pe, count):
        if count <= EARLY:
            pe.wait_ge(early_split, count)
        else:
            pe.wait_ge(split_done, count - EARLY)

    def pe_first(pe, g, u, par):
        e, k = divmod(u, CH)
        cols = slice(e * HID + k * P, e * HID + k * P + P)
        U = g * UNITS + u
        if u == 0:
            wait(pe, xsplit_ready, g + 1)
        if load and isinstance(g, int) and g == 0 and u % (2 * CH) == 0:
            split_upto(pe, part_at[0, u // (2 * CH)])
        for bank, w, ready, free in ((H1[u % 2], 1, h1_ready, silu_done),
                                     (H0[u % 2], 0, h0_ready, act_done)):
            if not (isinstance(U, int) and U < 2):
                wait(pe, free, U - 1)
            o = ps[:, bank, :]
            pe.matmul(o, w_hi[w][:, cols], x_hi[:, par, :], start=True, stop=False)
            pe.matmul(o, w_hi[w][:, cols], x_lo[:, par, :], start=False, stop=False)
            pe.matmul(o, w_lo[w][:, cols], x_hi[:, par, :], start=False, stop=True).then_inc(ready, 1)

    def pe_second(pe, g, u):
        U = g * UNITS + u
        o = ps[:, Y, :]
        if load and isinstance(g, int) and g == 0 and u % (2 * CH) == 0:
            split_upto(pe, part_at[2, u // (2 * CH)])
        if u == 0:
            wait(pe, gsplit_ready, g + 1)
            if not (isinstance(g, int) and g == 0):
                wait(pe, y_copied, g)
            pe.matmul(o, b2_st[:], g_st[:], start=True, stop=False)
        ws = slice(u * P, u * P + P)
        wait(pe, hi_done, U + 1)
        pe.matmul(o, w_hi[2][:, ws], act_hi[:, u % 4, :], start=False, stop=False)
        pe.matmul(o, w_lo[2][:, ws], act_hi[:, u % 4, :], start=False, stop=False)
        wait(pe, lo_done, U + 1)
        mm = pe.matmul(o, w_hi[2][:, ws], act_lo[:, u % 4, :], start=False, stop=(u == UNITS - 1))
        mm.then_inc(w2_done, 1)

    def pe_norm(pe, g):
        wait(pe, xn_ready, g + 1)
        wait(pe, xsplit_ready, g)
        for t in range(TG):
            mm = pe.transpose(ps[:, XT, t * P:(t + 1) * P], xn[:, t, :], ident[:])
        mm.then_inc(xT_ready, 1)

    def pe_logits(pe, g, par):
        wait(pe, xsplit_ready, g + 1)
        for t in range(TG):
            o = ps[:, LG, t * 2 * E:(t + 1) * 2 * E]
            pe.matmul(o, x_hi[:, par, t * P:(t + 1) * P], gw_hl[:], start=True, stop=False)
            mm = pe.matmul(o, x_lo[:, par, t * P:(t + 1) * P], gw_h0[:], start=False, stop=True)
        mm.then_inc(logits_ready, 1)

    def pe_gates(pe, g):
        wait(pe, gates_ready, g + 1)
        if not (isinstance(g, int) and g < 2):
            wait(pe, x_updated, g - 1)
        for t in range(TG):
            mm = pe.transpose(ps[:, GT, t * P:(t + 1) * P], gpad[:, t, :], ident[:])
        mm.then_inc(gT_ready, 1)

    def pe_close(pe, g):
        wait(pe, y_copied, g + 1)
        wait(pe, gsplit_ready, (g + 2) if not (isinstance(g, int) and g == GROUPS - 1) else g + 1)
        for t in range(TG):
            mm = pe.transpose(ps[:, GT, t * P:(t + 1) * P], y_sb[:, t * P:(t + 1) * P], ident[:])
        mm.then_inc(yT_ready, 1)

    def pe_group(pe, g, par, last):
        nxt = 1 - par
        for v in range(HEAD, UNITS + HEAD):
            if v < UNITS:
                pe_first(pe, g, v, par)
            elif not last:
                pe_first(pe, g + 1, v - UNITS, nxt)
            if v == HEAD:
                if not (isinstance(g, int) and g == 0):
                    pe_close(pe, g - 1)
                pe_second(pe, g, 0)
            if v - LAG < UNITS:
                pe_second(pe, g, v - LAG)
            if not last:
                if v == 4:
                    pe_norm(pe, g + 1)
                if v == LOGITS:
                    pe_logits(pe, g + 1, nxt)
                if v == GATES:
                    pe_gates(pe, g + 1)
            elif attn:
                attn["pe_before"](pe, v)
        if last:
            pe_close(pe, g)


    def act_unit(act, g, u):
        U = g * UNITS + u
        wait(act, h1_ready, U + 1)
        if not (isinstance(U, int) and U < 2):
            wait(act, gated_done, U - 1)
        nc.scalar.activation(silu[:, u % 2, :], ps[:, H1[u % 2], :], ACT.Silu,
                             bias=bias1[:, u:u + 1]).then_inc(silu_done, 1)

    def act_hi_part(act, g, u):
        U = g * UNITS + u
        wait(act, act_done, U + 1)
        if not (isinstance(U, int) and U < 4):
            wait(act, w2_done, U - 3)
        nc.scalar.activation(act_hi[:, u % 4, :], act_sb[:, u % 4, :], ACT.Copy).then_inc(hi_done, 1)

    def act_xhi(act, g, par):
        wait(act, xT_ready, g + 1)
        if not (isinstance(g, int) and g < 2):
            wait(act, h0_ready, (g - 1) * UNITS)
        nc.scalar.activation(x_hi[:, par, :], ps[:, XT, :], ACT.Copy).then_inc(xhi_done, 1)

    def act_tanh(act, g):
        wait(act, diff_ready, g + 1)
        nc.scalar.activation(th[:], diff[:], ACT.Tanh, scale=0.5).then_inc(tanh_ready, 1)

    def act_gf(act, g):
        wait(act, gT_ready, g + 1)
        if not (isinstance(g, int) and g == 0):
            wait(act, gates_out, g * 16)
        nc.scalar.activation(g_f, ps[0:E, GT, :], ACT.Copy).then_inc(gf_ready, 1)

    def act_y(act, g):
        wait(act, w2_done, (g + 1) * UNITS)
        if not (isinstance(g, int) and g == 0):
            wait(act, yT_ready, g)
        nc.scalar.activation(y_sb[:], ps[:, Y, :], ACT.Copy).then_inc(y_copied, 1)

    def act_split(act, k):
        if k < len(parts):
            full, hi, _, (loaded, count), _ = parts[k]
            act.wait_ge(loaded, 16 * count)
            nc.scalar.activation(hi, full, ACT.Copy).then_inc(whi_done, 1)

    def act_load(act):
        act.dma_start(xv(0), dram["x"][:, 0:2]).then_inc(x_loaded[0], 16)
        act.dma_start(gw[:], dram["gate_w"]).then_inc(router_loaded, 16)
        act.dma_start(gb[:], dram["gate_b"].partition_broadcast(P)).then_inc(router_loaded, 16)
        for dst, n in ((bias0[:], "b0"), (bias1[:], "b1")):
            act.dma_start(dst, dram[n]).then_inc(const_loaded, 16)

    def xv(g):
        return xs[:, g * TG:(g + 1) * TG, :].rearrange("p (b j) d -> p b j d", j=2)

    def act_group(act, g, last):
        for v in range(HEAD, UNITS + HEAD):
            if v == UNITS + LAG:
                act_y(act, g)
            if v < UNITS:
                act_unit(act, g, v)
            elif not last:
                act_unit(act, g + 1, v - UNITS)
            if v - 1 < UNITS:
                act_hi_part(act, g, v - 1)
            elif not last:
                act_hi_part(act, g + 1, v - 1 - UNITS)
            if load and isinstance(g, int) and g == 0 and v < UNITS:
                act_split(act, v + NEXT - 1)
            if not last:
                if v == 5:
                    act_xhi(act, g + 1, (g + 1) % 2)
                if v == LOGITS + 3:
                    act_tanh(act, g + 1)
                if v == GATES + 1:
                    act_gf(act, g + 1)
            elif attn:
                attn["act_before"](act, v)


    def pool_unit(pool, g, u, par):
        U = g * UNITS + u
        if not (isinstance(U, int) and U < 2):
            wait(pool, act_done, U - 1)
        if u in (0, FIRST * CH):
            wait(pool, gates_in[u > 0], (g + 1) * 16)
        wait(pool, silu_done, U + 1)
        nc.gpsimd.tensor_tensor(gated[:, u % 2, :], silu[:, u % 2, :], gates_bc[par][:, u // CH, :],
                                ALU.mult).then_inc(gated_done, 1)

    def pool_rstd(pool, g):
        wait(pool, stats_ready, g + 1)
        nc.gpsimd.tensor_tensor(vare[:], mv[:, :, 1], eps_sb[:], ALU.add).then_inc(rstd_step, 1)
        pool.wait_ge(rstd_step, 2 * g + 1)
        nc.gpsimd.tensor_tensor(rstd[:], vare[:], neg_half[:], ALU.pow).then_inc(rstd_step, 1)

    def pool_group(pool, g, par, last):
        for v in range(HEAD, UNITS + HEAD):
            if v < UNITS:
                pool_unit(pool, g, v, par)
            elif not last:
                pool_unit(pool, g + 1, v - UNITS, 1 - par)
            if v == STATS + 2 and not last:
                pool_rstd(pool, g + 2)
            if attn and isinstance(g, int) and g >= GROUPS - 2:
                if last:
                    attn["pool_before"](pool, v)
                else:
                    attn["pool_slot0"](pool, v - HEAD)


    def dve_unit(dve, g, u):
        U = g * UNITS + u
        wait(dve, h0_ready, U + 1)
        wait(dve, gated_done, U + 1)
        if not (isinstance(U, int) and U < 4):
            wait(dve, hi_done, U - 3)
            wait(dve, lo_done, U - 3)
        nc.vector.scalar_tensor_tensor(out=act_sb[:, u % 4, :], in0=ps[:, H0[u % 2], :],
                                       scalar=bias0[:, u:u + 1], in1=gated[:, u % 2, :],
                                       op0=ALU.add, op1=ALU.mult).then_inc(act_done, 1)

    def dve_lo_part(dve, g, u):
        U = g * UNITS + u
        wait(dve, hi_done, U + 1)
        if not (isinstance(U, int) and U < 4):
            wait(dve, w2_done, U - 3)
        nc.vector.tensor_tensor(act_lo[:, u % 4, :], act_sb[:, u % 4, :],
                                act_hi[:, u % 4, :].bitcast(F32), ALU.subtract).then_inc(lo_done, 1)

    def dve_stats(dve, g):
        gx = g % GROUPS
        if load and isinstance(g, int) and g < 3:
            dve.wait_ge(x_loaded[g], 16 if g < 2 else 16 * (GROUPS - 2))
            nc.vector.memset(spare[:, 0:1], 0.0)
        if not (isinstance(g, int) and g == 0):
            wait(dve, xn_ready, g)
        for t in range(TG):
            i = nc.vector.bn_stats(stats[:, t, :], xs[:, gx * TG + t, :])
        i.then_inc(bn_done, 1)
        dve.wait_ge(bn_done, g + 1)
        nc.vector.memset(spare[:, 0:1], 0.0)
        for t in range(TG):
            i = nc.vector.bn_aggr(mv[:, t, :], stats[:, t, :])
        i.then_inc(stats_ready, 1)

    def dve_norm(dve, g):
        wait(dve, rstd_step, 2 * g + 2)
        if not (isinstance(g, int) and g == 0):
            wait(dve, xT_ready, g)
        gx = g % GROUPS
        for t in range(TG):
            i = nc.vector.tensor_scalar(xn[:, t, :], xs[:, gx * TG + t, :], mv[:, t, 0:1],
                                        rstd[:, t:t + 1], ALU.subtract, ALU.mult)
        i.then_inc(xn_ready, 1)

    def dve_xsplit(dve, g, par):
        wait(dve, xhi_done, g + 1)
        nc.vector.tensor_tensor(x_lo[:, par, :], ps[:, XT, :], x_hi[:, par, :].bitcast(F32),
                                ALU.subtract).then_inc(xsplit_ready, 1)

    def dve_top(dve, g):
        wait(dve, logits_ready, g + 1)
        two = ps[:, LG, 0:TG * 2 * E].rearrange("p (t n e) -> p t n e", n=2, e=E)
        nc.vector.tensor_tensor(pre[:], two[:, :, 1], gb[:].unsqueeze(1).broadcast_to([P, TG, E]),
                                ALU.add).then_inc(pre_done, 1)
        dve.wait_ge(pre_done, g + 1)
        nc.vector.tensor_tensor(logits[:], two[:, :, 0], pre[:], ALU.add).then_inc(logits_done, 1)
        dve.wait_ge(logits_done, g + 1)
        nc.vector.memset(spare[:, 1:2], 0.0)
        for t in range(TG):
            i = nc.vector.max(top[:, t, :], logits[:, t, :])
        i.then_inc(top_done, 1)
        dve.wait_ge(top_done, g + 1)
        if not (isinstance(g, int) and g == 0):
            wait(dve, tanh_ready, g)
        nc.vector.tensor_tensor(diff[:], top[:, :, 0], top[:, :, 1], ALU.subtract).then_inc(diff_ready, 1)
        for t in range(TG):
            i = nc.vector.max_index(top_i[:, t, :], top[:, t, :], logits[:, t, :])
        i.then_inc(index_done, 1)
        dve.wait_ge(index_done, g + 1)
        nc.vector.tensor_copy(top_f[:], top_i[:, :, 0:2]).then_inc(topf_done, 1)

    def dve_gates(dve, g):
        wait(dve, tanh_ready, g + 1)
        nc.vector.tensor_scalar(w12[:, 0, :], th[:], 0.25, 0.25, ALU.mult, ALU.add)
        nc.vector.tensor_scalar(w12[:, 1, :], th[:], -0.25, 0.25, ALU.mult, ALU.add).then_inc(w12_done, 1)
        dve.wait_ge(topf_done, g + 1)
        for r in range(2):
            i = nc.vector.tensor_tensor(pick[:, r], iota[:].unsqueeze(1).broadcast_to([P, TG, E]),
                                        top_f[:, :, r:r + 1].broadcast_to([P, TG, E]), ALU.is_equal)
        i.then_inc(match_done, 1)
        dve.wait_ge(w12_done, g + 1)
        dve.wait_ge(match_done, g + 1)
        for r in range(2):
            i = nc.vector.tensor_tensor(pick[:, r], pick[:, r],
                                        w12[:, r, :].unsqueeze(2).broadcast_to([P, TG, E]), ALU.mult)
        i.then_inc(pick_done, 1)
        dve.wait_ge(pick_done, g + 1)
        if not (isinstance(g, int) and g == 0):
            wait(dve, gT_ready, g)
        stacked = gpad[:, :, 0:96].rearrange("p t (n e) -> p t n e", e=32)[:, :, :, 0:E]
        one, two = (pick[:, r].unsqueeze(2).broadcast_to([P, TG, 3, E]) for r in range(2))
        nc.vector.tensor_tensor(stacked, one, two, ALU.add).then_inc(gates_ready, 1)

    def dve_gsplit(dve, g):
        wait(dve, gf_ready, g + 1)
        if not (isinstance(g, int) and g == 0):
            wait(dve, w2_done, (g - 1) * UNITS + 1)
        nc.vector.tensor_copy(g_st[:], ps[:, GT, :]).then_inc(ghi_done, 1)
        dve.wait_ge(ghi_done, g + 1)
        nc.vector.tensor_tensor(g_st[32:64], ps[32:64, GT, :], g_st[32:64].bitcast(F32),
                                ALU.subtract).then_inc(gsplit_ready, 1)

    def dve_close(dve, g):
        wait(dve, yT_ready, g + 1)
        tiles = xs[:, g * TG:(g + 1) * TG, :] if isinstance(g, int) else xs[:, bass.ts(g, TG), :]
        nc.vector.tensor_tensor(tiles, tiles, ps[:, GT, :].rearrange("p (t d) -> p t d", d=P),
                                ALU.add).then_inc(x_updated, 1)

    def dve_split(dve, k):
        if k < len(parts):
            full, hi, lo, _, rows = parts[k]
            dve.wait_ge(whi_done, k + 1)
            nc.vector.tensor_tensor(lo[rows], full[rows], hi[rows].bitcast(F32), ALU.subtract).then_inc(split_done, 1)

    def dve_group(dve, g, last):
        for v in range(HEAD, UNITS + HEAD):
            if v < UNITS:
                dve_unit(dve, g, v)
            elif not last:
                dve_unit(dve, g + 1, v - UNITS)
            if v - 1 < UNITS:
                dve_lo_part(dve, g, v - 1)
            elif not last:
                dve_lo_part(dve, g + 1, v - 1 - UNITS)
            if v == HEAD and not (isinstance(g, int) and g == 0):
                dve_close(dve, g - 1)
            if load and isinstance(g, int) and g == 0 and v < UNITS:
                dve_split(dve, v + NEXT - 1)
            if not last:
                if v == 5:
                    dve_xsplit(dve, g + 1, (g + 1) % 2)
                if v == LOGITS + 0:
                    dve_top(dve, g + 1)
                if v == LOGITS + 2:
                    dve_gates(dve, g + 1)
                if v == GATES + 1:
                    dve_gsplit(dve, g + 1)
                if v == STATS:
                    dve_stats(dve, g + 2)
                if v == NORM:
                    dve_norm(dve, g + 2)
            elif attn:
                attn["dve_before"](dve, v, x_updated)
        if last:
            dve_close(dve, g)


    def sp_gates(sp, g):
        wait(sp, gf_ready, g + 1)
        sp.dma_start(gate_dram[g], g_f).then_inc(gates_out, 16)
        sp.wait_ge(gates_out, 16 * g + 16)
        wait(sp, gated_done, (g - 1) * UNITS)
        for part, es in enumerate((slice(0, FIRST), slice(FIRST, E))):
            sp.dma_start(gates_bc[g % 2][:, es, :],
                         gate_dram[g, es].partition_broadcast(P)).then_inc(gates_in[part], 16)

    def sp_store(sp, g):
        wait(sp, x_updated, g + 1)
        for j in range(T // S):
            b = g * (T // S) + j
            sp.dma_start(out_dram[:, b], xs[:, 2 * b:2 * b + 2, :]).then_inc(stored, 16)

    def sp_load_weights(sp, pairs):
        for q in pairs:
            cols = slice(q * 2 * HID, (q + 1) * 2 * HID)
            for w in (1, 0, 2):
                sp.dma_start(staged[w][:, cols], dram[f"w{w}"][:, cols]).then_inc(parts[part_at[w, q] - 1][3][0], 16)
                if (w, q) == (0, 0):
                    sp.wait_ge(b2_zero, 1)
                    for i in range(3):
                        sp.dma_start(b2_f[32 * i:32 * i + E, :], dram["b2"]).then_inc(b2_part[3][0], 16)
            if q == 0:
                sp.dma_start(xv(1), dram["x"][:, 2:4]).then_inc(x_loaded[1], 16)

    def sp_load_rest(sp):
        for g in range(2, GROUPS):
            sp.dma_start(xv(g), dram["x"][:, 2 * g:2 * g + 2]).then_inc(x_loaded[2], 16)
        sp.dma_start(bo_sb[:], dram["bo"].partition_broadcast(P)).then_inc(attn_loaded, 16)
        for dst, n in ((wqk_f[0:HALF, 0:HALF], "wk"), (wqk_f[HALF:P, 0:HALF], "wk"),
                       (wqk_f[0:HALF, HALF:P], "wq"), (wqk_f[HALF:P, HALF:P], "wq"),
                       (wv_f[0:HALF, :], "wv"), (wv_f[HALF:P, :], "wv"),
                       (wo_f[0:HALF, :], "wo"), (wo_f[HALF:P, :], "wo")):
            sp.dma_start(dst, dram[n]).then_inc(attn_loaded, 16)

    def pe_head(pe, s, k, max_done):
        if (s, k) == (NB, 1):
            wait(pe, max_done, NB * NH)
            pe_norm(pe, 0)
        if (s, k) == (NB, 4):
            pe_logits(pe, 0, 0)
        if (s, k) == (NB, 12):
            pe_gates(pe, 0)

    def act_head(act, s, k):
        if (s, k) == (NB, 1):
            act_xhi(act, 0, 0)
        if (s, k) == (NB, 8):
            act_tanh(act, 0)
        if (s, k) == (NB, 13):
            act_gf(act, 0)

    def pool_head(pool, s):
        if s in (NB, NB + 1):
            pool_rstd(pool, s - NB)

    def dve_head(dve, s, k, cols_ready, attn_updated):
        if (s, k) == (NB - 1, 12):
            wait(dve, cols_ready, NH * (NB - 3))
            nc.vector.memset(gpad, 0.0).then_inc(gpad_zero, 1)
            wait(dve, attn_updated, 4)
            nc.vector.memset(spare[:, 0:1], 0.0)
            dve_stats(dve, 0)
        if (s, k) == (NB, 0):
            dve_norm(dve, 0)
        if (s, k) == (NB, 2):
            dve_xsplit(dve, 0, 0)
        if (s, k) == (NB, 6):
            dve_top(dve, 0)
        if (s, k) == (NB, 9):
            dve.wait_ge(gpad_zero, 1)
            dve_gates(dve, 0)
        if (s, k) == (NB, 11):
            dve_stats(dve, 1)
        if (s, k) == (NB, 14):
            dve_gsplit(dve, 0)
        if (s, k) == (NB + 1, 2):
            dve_norm(dve, 1)

    def sp_head(sp):
        sp_gates(sp, 0)

    def run():
        nonlocal silu, gated, act_sb, act_hi, act_lo, y_sb
        with ExitStack() as late:
            def sb(n, shape, dt=F32):
                return late.enter_context(nc.sbuf_tensor(f"{name}_{n}", shape, dt))

            gates_bc.append(sb("gates_bc1", [P, E, T]))
            silu = sb("silu", [P, 2, T])
            gated = sb("gated", [P, 2, T])
            act_sb = sb("act", [P, 4, T])
            act_hi, act_lo = sb("act_hi", [P, 4, T], F32R), sb("act_lo", [P, 4, T], F32R)
            y_sb = sb("y_sb", [P, T])
            block = late.enter_context(nc.Block())

            @block.tensor
            def _(pe):
                if load:
                    pe.wait_ge(ident_step, 3)
                    pe_norm(pe, 0)
                    pe.wait_ge(router_split, 1)
                    pe_logits(pe, 0, 0)
                    pe_gates(pe, 0)
                for u in range(HEAD):
                    pe_first(pe, 0, u, 0)
                pe_group(pe, 0, 0, False)
                pe_group(pe, 1, 1, False)
                with pe.Fori(1, GROUPS // 2 - 1) as turn:
                    pe_group(pe, 2 * turn, 0, False)
                    pe_group(pe, 2 * turn + 1, 1, False)
                pe_group(pe, GROUPS - 2, 0, False)
                pe_group(pe, GROUPS - 1, 1, True)

            @block.scalar
            def _(act):
                if load:
                    act_load(act)
                    act.wait_ge(router_loaded, 2 * 16)
                    act.wait_ge(gpad_zero, 1)
                    nc.scalar.activation(gw_hl[:, 0:E], gw[:], ACT.Copy).then_inc(router_hi, 1)
                    nc.scalar.activation(gw_h0[:, 0:E], gw[:], ACT.Copy).then_inc(router_hi, 1)
                    nc.scalar.activation(gw_h0[:, E:2 * E], gpad[:, 0, 0:E], ACT.Copy).then_inc(router_hi, 1)
                    act_xhi(act, 0, 0)
                    for k in range(EARLY):
                        act_split(act, k)
                    act_tanh(act, 0)
                    act_gf(act, 0)
                    for k in range(EARLY, NEXT):
                        act_split(act, k)
                    act.wait_ge(const_loaded, 2 * 16)
                for u in range(HEAD):
                    act_unit(act, 0, u)
                    if u:
                        act_hi_part(act, 0, u - 1)
                        if load:
                            act_split(act, NEXT + u - 1)
                act_group(act, 0, False)
                with act.Fori(1, GROUPS - 1) as g:
                    act_group(act, g, False)
                act_group(act, GROUPS - 1, True)

            @block.gpsimd
            def _(pool):
                if load:
                    nc.gpsimd.memset(ident[:], 0.0).then_inc(ident_step, 1)
                    nc.gpsimd.iota(iota_i[:], pattern=[[1, E]], base=0, channel_multiplier=0).then_inc(ident_step, 1)
                    pool.wait_ge(ident_step, 2)
                    nc.gpsimd.affine_select(out=ident[:], in_=ident[:], compare_op=ALU.not_equal, fill=1.0, base=0,
                                            pattern=[[-1, P]], channel_multiplier=1).then_inc(ident_step, 1)
                    pool.wait_ge(const_made, 2)
                    pool_rstd(pool, 0)
                    pool_rstd(pool, 1)
                    for k in range(EARLY):
                        full, hi, lo, _, rows = parts[k]
                        pool.wait_ge(whi_done, k + 1)
                        if k:
                            pool.wait_ge(early_split, k)
                        nc.gpsimd.tensor_tensor(lo[rows], full[rows], hi[rows].bitcast(F32), ALU.subtract).then_inc(early_split, 1)
                for u in range(HEAD):
                    pool_unit(pool, 0, u, 0)
                with pool.Fori(0, GROUPS // 2 - 1) as turn:
                    pool_group(pool, 2 * turn, 0, False)
                    pool_group(pool, 2 * turn + 1, 1, False)
                pool_group(pool, GROUPS - 2, 0, False)
                pool_group(pool, GROUPS - 1, 1, True)

            @block.vector
            def _(dve):
                if load:
                    nc.vector.memset(b2_f[:], 0.0).then_inc(b2_zero, 1)
                    nc.vector.memset(neg_half[:], -0.5).then_inc(const_made, 1)
                    nc.vector.memset(eps_sb[:], EPS).then_inc(const_made, 1)
                    nc.vector.memset(gpad, 0.0).then_inc(gpad_zero, 1)
                    dve_stats(dve, 0)
                    dve_norm(dve, 0)
                    dve_stats(dve, 1)
                    dve.wait_ge(router_hi, 3)
                    nc.vector.tensor_tensor(gw_hl[:, E:2 * E], gw[:], gw_hl[:, 0:E].bitcast(F32),
                                            ALU.subtract).then_inc(router_split, 1)
                    dve_xsplit(dve, 0, 0)
                    dve.wait_ge(ident_step, 3)
                    nc.vector.tensor_copy(identb[:], ident[:])
                    nc.vector.tensor_copy(iota[:], iota_i[:])
                    dve.wait_ge(router_loaded, 2 * 16)
                    dve_top(dve, 0)
                    dve.wait_ge(gpad_zero, 1)
                    dve_gates(dve, 0)
                    dve_gsplit(dve, 0)
                    dve_norm(dve, 1)
                    for k in range(EARLY, NEXT):
                        dve_split(dve, k)
                    dve.wait_ge(const_loaded, 2 * 16)
                for u in range(HEAD):
                    dve_unit(dve, 0, u)
                    if u:
                        dve_lo_part(dve, 0, u - 1)
                        if load:
                            dve_split(dve, NEXT + u - 1)
                dve_group(dve, 0, False)
                with dve.Fori(1, GROUPS - 1) as g:
                    dve_group(dve, g, False)
                dve_group(dve, GROUPS - 1, True)

            @block.sync
            def _(sp):
                if load:
                    sp_load_weights(sp, (0, 1, 2))
                    sp_gates(sp, 0)
                    sp_load_weights(sp, (3,))
                    sp_load_rest(sp)
                for g in range(GROUPS + 1):
                    if 0 < g < GROUPS:
                        sp_gates(sp, g)
                    if g and out_dram is not None:
                        sp_store(sp, g - 1)
                if out_dram is not None:
                    sp.wait_ge(stored, 16 * NB)
                if attn:
                    attn["sp_before"](sp)

    return dict(pe_head=pe_head, act_head=act_head, pool_head=pool_head, dve_head=dve_head,
                           sp_head=sp_head, run=run)


def attention(nc, c, xs, ident, identb, wqk_hi, wqk_lo, wv_hi, wv_lo, wo_hi, wo_lo, bo_sb, eps_sb,
              neg_half, kq_dram, ps, stage):
    NJ = 4
    HG = NH // NJ
    KP, KM = 24, 27
    SCALE = float(P // NH) ** -0.5
    UR = NH
    SBK, O, MISC_A, MISC_B = (3, 4), 5, 6, 7
    SA = (0, 1, 2) * 5 + (1,)

    def sb(n, shape, dt=F32):
        return c.enter_context(nc.sbuf_tensor(f"attn_{n}", shape, dt))

    def sem(n):
        return c.enter_context(nc.semaphore(f"attn_{n}"))

    qa, ka = ([stage[i].bitcast(BF16).rearrange("p (h t) -> p h t", h=NH)] for i in range(2))
    va = [sb("va0", [P, 2, NH, 32])]
    ones_rows = sb("ones_rows", [3, S], BF16)
    stats, mv = sb("stats", [P, 2, 6]), sb("mv", [P, 2, 2])
    vare, rstd = sb("vare", [P, 2]), sb("rstd", [P, 2])
    xn = sb("xn", [P, 2, 2, HALF])
    xT = sb("xT", [P, S], F32R)
    kqp = sb("kqp", [P, 3, S], BF16)
    rem = sb("rem", [P, S])
    spare = sb("spare", [P, 1])
    after = pt = nm = nmr = mp = mT = oT = rsum = otok = osp = oTs = None

    mp_zero, zeros_out, slot0_zeroed = sem("mp_zero"), sem("zeros_out"), sem("slot0_zeroed")
    zeroed, ones_made, ones_in, v_init = sem("zeroed"), sem("ones_made"), sem("ones_in"), sem("v_init")
    bn_done, stats_ready, rstd_step, xn_ready = sem("bn_done"), sem("stats_ready"), sem("rstd_step"), sem("xn_ready")
    xT_ready, xhi_done, xT_split = sem("xT_ready"), sem("xhi_done"), sem("xT_split")
    proj_ready, p0_done, v_copied = sem("proj_ready"), sem("p0_done"), sem("v_copied")
    rem_done, p1_done, pieces_ready = sem("rem_done"), sem("p1_done"), sem("pieces_ready")
    pieces_out, ops_in = sem("pieces_out"), sem("ops_in")
    rows_ready, max_done = sem("rows_ready"), sem("max_done")
    m0_done, mr_done, m1_done, m_ready = sem("m0_done"), sem("mr_done"), sem("m1_done"), sem("m_ready")
    mT_ready, mT_copied, m_in = sem("mT_ready"), sem("mT_copied"), sem("m_in")
    cols_ready, exp_done, pv_done = sem("cols_ready"), sem("exp_done"), sem("pv_done")
    oT_copied, otok_ready, recip_done, norm_done = sem("oT_copied"), sem("otok_ready"), sem("recip_done"), sem("norm_done")
    ohi_done, osp_ready, oTs_ready, oTs_copied = sem("ohi_done"), sem("osp_ready"), sem("oTs_ready"), sem("oTs_copied")
    y_ready, x_updated, bias_added = sem("y_ready"), sem("x_updated"), sem("bias_added")

    def first(v, n=1):
        return isinstance(v, int) and v < n

    def valid(b):
        return not isinstance(b, int) or 0 <= b < NB

    def run_steps(eng, step):
        for s in range(4):
            step(eng, s, s % 4)
        with eng.Fori(1, 3) as turn:
            for i in range(4):
                step(eng, turn * 4 + i, i)
        for s in range(12, NB + 3):
            step(eng, s, s % 4)

    SHIFT = 16
    AT = dict(project=3, xT=8, mT=2, otok1=6, oTs=10, out=12, otok0=11, values3=1, values0=5)
    LATE = dict(otok1=3, oTs=3, out=3, otok0=2)

    def late(s, sl, k):
        return (s, sl, k - SHIFT + UR) if k < SHIFT else (s + 1, (sl + 1) % 4, k - SHIFT)

    def unit(name):
        return (AT[name] + SHIFT) % UR if name in LATE else AT[name]

    def batch(s, name):
        if name in LATE:
            return s - LATE[name] + (AT[name] + SHIFT < UR)
        return s + dict(project=1, xT=2, mT=-1)[name]

    def misc_uses(s, bank):
        uses = []
        for name in sorted(("project", "xT", "otok0") if bank == MISC_A else ("mT", "otok1", "oTs", "out"),
                           key=lambda n: (unit(n), n in LATE)):
            b = batch(s, name)
            semaphore = dict(project=rem_done, xT=xT_split, otok0=norm_done, mT=mT_copied, otok1=norm_done,
                             oTs=oTs_copied, out=x_updated)[name]
            value = dict(otok0=2 * b + 1, otok1=2 * b + 2).get(name, b + 1)
            uses.append((name, b, semaphore, value))
        return [u for u in uses if valid(u[1])]

    def misc_free(eng, b, bank, name):
        s = b - batch(0, name)
        before = misc_uses(s - 1, bank)
        uses = before + misc_uses(s, bank)
        at = len(before) + [u[0] for u in misc_uses(s, bank)].index(name)
        if at:
            _, _, semaphore, value = uses[at - 1]
            wait(eng, semaphore, value)

    def pe_cols(pe, b, sl, h):
        n = NH * b + h
        if h == 0:
            wait(pe, m_in, 48 * (b + 1))
        if not first(n, 2):
            wait(pe, exp_done, n - 1)
        for kc in range(2):
            mm = pe.matmul(ps[:, SBK[h % 2], kc * S:(kc + 1) * S], ka[sl][:, h, kc * P:(kc + 1) * P],
                           qa[sl][:, h, :], start=True, stop=True)
        mm.then_inc(cols_ready, 1)

    def pe_rows(pe, b, sl, k):
        pair, qc = divmod(k, 2)
        if k == 0:
            wait(pe, ops_in, 16 * 6 * (b + 1))
            if first(b, 4):
                wait(pe, ones_in, 16 * (b + 1))
        ago = (SA[:k][::-1] + SA[::-1]).index(SA[k]) + 1
        n = UR * b + k
        if not first(n, ago):
            wait(pe, max_done, n - ago + 1)
        for j in range(2):
            h = 2 * pair + j
            mm = pe.matmul(ps[:, SA[k], j * S:(j + 1) * S],
                           qa[sl][:, h, qc * P:(qc + 1) * P], ka[sl][:, h, :], start=True, stop=True)
        mm.then_inc(rows_ready, 1)

    def pe_values(pe, b, sl, g):
        if g == 0:
            wait(pe, v_copied, b + 1)
        wait(pe, exp_done, NH * b + NJ * (g + 1))
        if g % 2 == 0 and not first(HG * b + g, 2):
            wait(pe, oT_copied, 2 * b + g // 2)
        for kc in range(2):
            for j in range(NJ):
                mm = pe.matmul(ps[32 * j:32 * j + 32, O, (g % 2) * S:(g % 2 + 1) * S],
                               va[sl][:, kc, NJ * g + j, :], pt[:, g % 2, j, kc * S:(kc + 1) * S],
                               start=(kc == 0), stop=(kc == 1), tile_position=(0, 32 * j))
        mm.then_inc(pv_done, 1)

    def pe_xT(pe, b):
        wait(pe, xn_ready, b + 1)
        misc_free(pe, b, MISC_A, "xT")
        for j in range(2):
            mm = pe.transpose(ps[:, MISC_A, j * P:(j + 1) * P], xn[:, j].rearrange("p a d -> p (a d)"), ident[:])
        mm.then_inc(xT_ready, 1)

    def pe_mT(pe, b):
        wait(pe, m_ready, b + 1)
        misc_free(pe, b, MISC_B, "mT")
        for qc in range(2):
            mm = pe.transpose(ps[:, MISC_B, qc * HALF:(qc + 1) * HALF].bitcast(BF16),
                              mp[:, qc].rearrange("p a h -> p (a h)"), identb[:])
        mm.then_inc(mT_ready, 1)

    def pe_project(pe, b):
        wait(pe, xT_split, b + 1)
        misc_free(pe, b, MISC_A, "project")
        pe.matmul(ps[:, MISC_A, 0:S], wqk_hi[:], xT[:], start=True, stop=False, skip_group_check=True)
        pe.matmul(ps[:, MISC_A, 0:S], wqk_lo[:], xT[:], start=False, stop=True, skip_group_check=True)
        for j in range(2):
            o = ps[:, MISC_A, S + j * HALF:S + (j + 1) * HALF]
            pe.matmul(o, xT[:, j * P:(j + 1) * P], wv_hi[:], start=False, stop=False, skip_group_check=True)
            mm = pe.matmul(o, xT[:, j * P:(j + 1) * P], wv_lo[:], start=False, stop=True, skip_group_check=True)
        mm.then_inc(proj_ready, 1)

    MISC_OTOK = (MISC_A, MISC_B)

    def pe_otok(pe, b, pair):
        wait(pe, oT_copied, 2 * b + pair + 1)
        misc_free(pe, b, MISC_OTOK[pair], f"otok{pair}")
        for g in range(2):
            for qc in range(2):
                mm = pe.transpose(ps[:, MISC_OTOK[pair], (2 * qc + g) * P:(2 * qc + g + 1) * P],
                                  oT[:, g * S + qc * P:g * S + (qc + 1) * P], ident[:])
        mm.then_inc(otok_ready, 1)

    def pe_oTs(pe, b):
        wait(pe, osp_ready, b + 1)
        misc_free(pe, b, MISC_B, "oTs")
        for qc in range(2):
            mm = pe.transpose(ps[:, MISC_B, qc * P:(qc + 1) * P], osp[:, qc].rearrange("p a d -> p (a d)"), ident[:])
        mm.then_inc(oTs_ready, 1)

    def pe_out(pe, b):
        wait(pe, oTs_copied, b + 1)
        misc_free(pe, b, MISC_B, "out")
        for qc in range(2):
            o = ps[:, MISC_B, qc * P:(qc + 1) * P]
            pe.matmul(o, oTs[:, qc * P:(qc + 1) * P], wo_hi[:], start=True, stop=False)
            mm = pe.matmul(o, oTs[:, qc * P:(qc + 1) * P], wo_lo[:], start=False, stop=True)
        mm.then_inc(y_ready, 1)

    def pe_step(pe, s, sl):
        for k in range(UR):
            ls, lsl, lk = late(s, sl, k)
            if valid(ls - 2):
                pe_cols(pe, ls - 2, (lsl - 2) % 4, lk)
            if k == AT["project"] and valid(s + 1):
                pe_project(pe, s + 1)
            if k == AT["mT"] and valid(s - 1):
                pe_mT(pe, s - 1)
            if k == AT["xT"] and valid(s + 2):
                pe_xT(pe, s + 2)
            if lk == AT["otok1"] and valid(ls - 3):
                pe_otok(pe, ls - 3, 1)
            if lk == AT["oTs"] and valid(ls - 3):
                pe_oTs(pe, ls - 3)
            if lk == AT["out"] and valid(ls - 3):
                pe_out(pe, ls - 3)
            if lk == AT["otok0"] and valid(ls - 2):
                pe_otok(pe, ls - 2, 0)
            if valid(s):
                pe_rows(pe, s, sl, k)
            if lk == AT["values3"] and valid(ls - 3):
                pe_values(pe, ls - 3, (lsl - 3) % 4, 3)
            if lk - AT["values0"] in (0, NJ, 2 * NJ) and valid(ls - 2):
                pe_values(pe, ls - 2, (lsl - 2) % 4, (lk - AT["values0"]) // NJ)
            if isinstance(s, int):
                after["pe_head"](pe, s, k, max_done)

    def act_exp(act, b, h):
        g, j = divmod(h, NJ)
        if j == 0 and not first(HG * b + g, 2):
            wait(act, pv_done, HG * b + g - 1)
        wait(act, cols_ready, NH * b + h + 1)
        nc.scalar.activation(pt[:, g % 2, j, :], ps[:, SBK[h % 2], :], ACT.Exp, scale=SCALE).then_inc(exp_done, 1)

    def act_xhi(act, b):
        wait(act, xT_ready, b + 1)
        if not first(b):
            wait(act, proj_ready, b)
        nc.scalar.activation(xT[:], ps[:, MISC_A, 0:S], ACT.Copy).then_inc(xhi_done, 1)

    def act_mT(act, b):
        wait(act, mT_ready, b + 1)
        if not first(b):
            wait(act, m_in, 48 * b)
        nc.scalar.activation(mT[:], ps[0:3 * NH, MISC_B, 0:P].bitcast(BF16), ACT.Copy).then_inc(mT_copied, 1)

    def act_project(act, b, sl):
        wait(act, proj_ready, b + 1)
        if not first(b):
            wait(act, pieces_out, 16 * b)
        nc.scalar.activation(kqp[:, 0, :], ps[:, MISC_A, 0:S], ACT.Copy).then_inc(p0_done, 1)
        if not first(b, 4):
            wait(act, pv_done, HG * (b - 3))
        else:
            wait(act, v_init, 2 * b + 2)
        nc.scalar.activation(va[sl][:, :, :, 0:DH],
                             ps[:, MISC_A, S:S + 2 * HALF].rearrange("p (c h d) -> p c h d", c=2, d=DH),
                             ACT.Copy).then_inc(v_copied, 1)

    def act_oT(act, b, pair):
        wait(act, pv_done, HG * b + 2 * pair + 2)
        if not first(2 * b + pair):
            wait(act, otok_ready, 2 * b + pair)
        nc.scalar.activation(oT[:], ps[:, O, :], ACT.Copy).then_inc(oT_copied, 1)

    def act_oTs(act, b):
        wait(act, oTs_ready, b + 1)
        if not first(b):
            wait(act, y_ready, b)
        nc.scalar.activation(oTs[:], ps[:, MISC_B, 0:S], ACT.Copy).then_inc(oTs_copied, 1)

    def act_piece1(act, b):
        wait(act, rem_done, b + 1)
        nc.scalar.activation(kqp[:, 1, :], rem[:], ACT.Copy).then_inc(p1_done, 1)

    def act_step(act, s, sl):
        for k in range(UR):
            ls, lsl, lk = late(s, sl, k)
            if lk == 2 and valid(ls - 3):
                act_oT(act, ls - 3, 1)
            if lk == 10 and valid(ls - 2):
                act_oT(act, ls - 2, 0)
            if valid(ls - 2):
                act_exp(act, ls - 2, lk)
            if k == 3 and valid(s + 1):
                act_project(act, s + 1, (sl + 1) % 4)
            if k == 3 and valid(s - 1):
                act_mT(act, s - 1)
            if k == 4 and valid(s + 1):
                act_piece1(act, s + 1)
            if k == 8 and valid(s + 2):
                act_xhi(act, s + 2)
            if lk == 10 and valid(ls - 3):
                act_oTs(act, ls - 3)
            if isinstance(s, int):
                after["act_head"](act, s, k)

    def pool_rstd(pool, b):
        wait(pool, stats_ready, b + 1)
        nc.gpsimd.tensor_tensor(vare[:], mv[:, :, 1], eps_sb[:, 0:2], ALU.add).then_inc(rstd_step, 1)
        pool.wait_ge(rstd_step, 2 * b + 1)
        nc.gpsimd.tensor_tensor(rstd[:], vare[:], neg_half[:, 0:2], ALU.pow).then_inc(rstd_step, 1)

    def tiles(b):
        return xs[:, 2 * b:2 * b + 2, :] if isinstance(b, int) else xs[:, bass.ts(b, 2), :]

    def pool_bias(pool, b):
        wait(pool, xn_ready, b + 1)
        nc.gpsimd.tensor_tensor(tiles(b), tiles(b), bo_sb[:].unsqueeze(1).broadcast_to([P, 2, P]),
                                ALU.add).then_inc(bias_added, 1)

    def pool_olow(pool, b):
        wait(pool, ohi_done, b + 1)
        if not first(b):
            wait(pool, oTs_ready, b)
        nc.gpsimd.tensor_tensor(osp[:, :, 1, :], otok[:], osp[:, :, 0, :], ALU.subtract).then_inc(osp_ready, 1)

    def pool_piece2(pool, b):
        wait(pool, p1_done, b + 1)
        nc.gpsimd.tensor_tensor(kqp[:, 2, :], rem[:], kqp[:, 1, :], ALU.subtract).then_inc(pieces_ready, 1)

    def pool_values_init(pool, i):
        pool.memset(va[i][:], 0.0).then_inc(v_init, 1)
        pool.wait_ge(v_init, 2 * i + 1)
        pool.memset(va[i][:, :, :, DH:DH + 1], 1.0).then_inc(v_init, 1)

    def pool_slot_init(pool, i):
        pool.memset(qa[i].bitcast(U32), 0).then_inc(zeroed, 1)
        pool.memset(ka[i].bitcast(U32), 0).then_inc(zeroed, 1)
        pool_values_init(pool, i)

    OLOW = -batch(0, "otok1")

    def pool_step(pool, s, sl):
        if isinstance(s, int) and s >= NB:
            after["pool_head"](pool, s)
        if valid(s + 2):
            pool_rstd(pool, s + 2)
        if valid(s + 1):
            pool_piece2(pool, s + 1)
        if first(s, 2):
            pool_slot_init(pool, s + 2)
        if valid(s + 2):
            pool_bias(pool, s + 2)
        if valid(s - OLOW):
            pool_olow(pool, s - OLOW)


    def dve_stats(dve, b):
        if not first(b):
            wait(dve, xn_ready, b)
        for j in range(2):
            i = nc.vector.bn_stats(stats[:, j, :], xs[:, 2 * b + j, :])
        i.then_inc(bn_done, 1)
        wait(dve, bn_done, b + 1)
        nc.vector.memset(spare[:], 0.0)
        for j in range(2):
            i = nc.vector.bn_aggr(mv[:, j, :], stats[:, j, :])
        i.then_inc(stats_ready, 1)

    def dve_norm(dve, b):
        wait(dve, rstd_step, 2 * b + 2)
        if not first(b):
            wait(dve, xT_ready, b)
        for j in range(2):
            i = nc.vector.tensor_scalar(xn[:, j], xs[:, 2 * b + j, 0:HALF].unsqueeze(1).broadcast_to([P, 2, HALF]),
                                        mv[:, j, 0:1], rstd[:, j:j + 1], ALU.subtract, ALU.mult)
        i.then_inc(xn_ready, 1)

    def dve_xlo(dve, b):
        wait(dve, xhi_done, b + 1)
        nc.vector.tensor_tensor(xT[HALF:P, :], ps[HALF:P, MISC_A, 0:S], xT[HALF:P, :].bitcast(F32),
                                ALU.subtract).then_inc(xT_split, 1)

    def dve_rem(dve, b):
        wait(dve, v_copied, b + 1)
        if not first(b):
            wait(dve, pieces_ready, b)
        nc.vector.tensor_tensor(rem[:], ps[:, MISC_A, 0:S], kqp[:, 0, :], ALU.subtract).then_inc(rem_done, 1)

    def dve_max(dve, b, k):
        pair, qc = divmod(k, 2)
        wait(dve, rows_ready, UR * b + k + 1)
        if k == 0 and first(b):
            dve.wait_ge(mp_zero, 1)
        elif k == 0:
            wait(dve, m_ready, b)
        nc.vector.tensor_reduce(nm[:, qc, 2 * pair:2 * pair + 2],
                                ps[:, SA[k], :].rearrange("p (j t) -> p j t", t=S),
                                AX.X, ALU.max, negate=True).then_inc(max_done, 1)

    def dve_m(dve, b):
        wait(dve, max_done, UR * (b + 1))
        if not first(b):
            wait(dve, mT_ready, b)
        nc.vector.tensor_copy(mp[:, :, 0, :], nm[:]).then_inc(m0_done, 1)
        wait(dve, m0_done, b + 1)
        nc.vector.tensor_tensor(nmr[:], nm[:], mp[:, :, 0, :], ALU.subtract).then_inc(mr_done, 1)
        wait(dve, mr_done, b + 1)
        nc.vector.tensor_copy(mp[:, :, 1, :], nmr[:]).then_inc(m1_done, 1)
        wait(dve, m1_done, b + 1)
        nc.vector.tensor_tensor(mp[:, :, 2, :], nmr[:], mp[:, :, 1, :], ALU.subtract).then_inc(m_ready, 1)

    def dve_otok(dve, b, pair):
        n = 2 * b + pair
        wait(dve, otok_ready, n + 1)
        o = ps[:, MISC_OTOK[pair], :].rearrange("p (c h k) -> p c h k", c=2, k=32)
        if not first(n):
            wait(dve, norm_done, n)
        nc.vector.reciprocal(rsum[:].rearrange("p c g j -> p c (g j)"), o[:, :, :, DH]).then_inc(recip_done, 1)
        wait(dve, recip_done, n + 1)
        if pair == 0 and not first(b):
            wait(dve, osp_ready, b)
        nc.vector.tensor_tensor(
            otok[:, :, pair * 32:pair * 32 + 32].rearrange("p c (h d) -> p c h d", d=DH), o[:, :, :, 0:DH],
            rsum[:].rearrange("p c g j -> p c (g j)").unsqueeze(3).broadcast_to([P, 2, 2 * NJ, DH]),
            ALU.mult).then_inc(norm_done, 1)

    def dve_ohi(dve, b):
        wait(dve, norm_done, 2 * b + 2)
        if not first(b):
            wait(dve, oTs_ready, b)
        nc.vector.tensor_copy(osp[:, :, 0, :].bitcast(F32R), otok[:]).then_inc(ohi_done, 1)

    def dve_residual(dve, b):
        wait(dve, y_ready, b + 1)
        wait(dve, bias_added, b + 1)
        t = tiles(b)
        nc.vector.tensor_tensor(t, t, ps[:, MISC_B, 0:S].rearrange("p (t d) -> p t d", d=P), ALU.add).then_inc(x_updated, 1)

    def dve_step(dve, s, sl):
        for k in range(UR):
            ls, lsl, lk = late(s, sl, k)
            if k == 4 and valid(s + 1):
                dve_rem(dve, s + 1)
            if valid(s):
                dve_max(dve, s, k)
            if k == 2 and valid(s + 2):
                dve_stats(dve, s + 2)
            if k == 5 and valid(s + 2):
                dve_norm(dve, s + 2)
            if k == 7 and valid(s + 2):
                dve_xlo(dve, s + 2)
            if lk == 6 and valid(ls - 3):
                dve_otok(dve, ls - 3, 1)
                dve_ohi(dve, ls - 3)
            if lk == 12 and valid(ls - 3):
                dve_residual(dve, ls - 3)
            if lk == 10 and valid(ls - 2):
                dve_otok(dve, ls - 2, 0)
            if k == UR - 1 and valid(s):
                dve_m(dve, s)
            if isinstance(s, int):
                after["dve_head"](dve, s, k, cols_ready, x_updated)

    def sp_constant_rows(sp, i):
        if i == 0:
            sp.wait_ge(slot0_zeroed, 8)
        else:
            sp.wait_ge(zeroed, 2 * i)
        sp.dma_start(ka[i][KP:KM], ones_rows[:].unsqueeze(1).broadcast_to([3, NH, S])).then_inc(ones_in, 16)

    def sp_pieces(sp, b):
        if b == 0:
            sp_constant_rows(sp, 0)
        wait(sp, pieces_ready, b + 1)
        sp.dma_start(kq_dram[b, 0:3].rearrange("a i c t -> (i c) a t"), kqp[:]).then_inc(pieces_out, 16)

    def sp_operands(sp, b, sl):
        if first(b, 4):
            if b:
                sp_constant_rows(sp, b)
        else:
            wait(sp, cols_ready, NH * (b - 3))
        wait(sp, pieces_out, 16 * (b + 1))
        kq = kq_dram[b].rearrange("a i (d h) t -> a i d (h t)", d=DH)
        kv, qv = (t[sl].rearrange("p h t -> p (h t)") for t in (ka, qa))
        r = 0
        for n in (3, 2, 1):
            sp.dma_start(kv[r:r + n * DH, :], kq[0:n, 0]).then_inc(ops_in, 16)
            r += n * DH
        r = 0
        for piece, n in enumerate((3, 2)):
            sp.dma_start(qv[r:r + n * DH, :], kq[piece, 1].unsqueeze(0).broadcast_to([n, DH, NH * S])).then_inc(ops_in, 16)
            r += n * DH
        rows = kq_dram[b].rearrange("a i (d h) t -> (a i d) (h t)", d=DH)
        sp.dma_start(qv[r:KM, :], rows[5 * DH:5 * DH + KM - r]).then_inc(ops_in, 16)

    def sp_max(sp, b, sl):
        wait(sp, mT_copied, b + 1)
        for i in range(3):
            sp.dma_start(qa[sl][KP + i:KP + i + 1], mT[NH * i:NH * i + NH, :]).then_inc(m_in, 16)

    def sp_step(sp, s, sl):
        if valid(s - 1):
            sp_max(sp, s - 1, (sl - 1) % 4)
        if valid(s + 1):
            sp_pieces(sp, s + 1)
            sp_operands(sp, s + 1, (sl + 1) % 4)

    def pe_before(pe, v):
        if v == 10:
            pe_xT(pe, 0)
        if v == 12:
            pe_project(pe, 0)
        if v == 17:
            pe_xT(pe, 1)

    def act_before(act, v):
        if v == 10:
            act_xhi(act, 0)
        if v == 12:
            act_project(act, 0, 0)
        if v == 14:
            act_piece1(act, 0)
        if v == 17:
            act_xhi(act, 1)

    def dve_before(dve, v, x_updated):
        if v == 5:
            wait(dve, x_updated, 1)
            dve_stats(dve, 0)
        if v == 8:
            dve_norm(dve, 0)
        if v == 10:
            dve_xlo(dve, 0)
        if v == 11:
            dve_stats(dve, 1)
        if v == 13:
            dve_rem(dve, 0)
        if v == 15:
            dve_norm(dve, 1)
        if v == 17:
            dve_xlo(dve, 1)

    def pool_slot0(pool, k):
        quarter = NH // 4
        if k < 4:
            pool.memset(qa[0][:, k * quarter:(k + 1) * quarter].bitcast(U32), 0).then_inc(slot0_zeroed, 1)
        elif k < 8:
            pool.memset(ka[0][:, (k - 4) * quarter:(k - 3) * quarter].bitcast(U32), 0).then_inc(slot0_zeroed, 1)
        if k == 8:
            pool_values_init(pool, 0)
        if k == 9:
            pool.memset(ones_rows[:], 1.0).then_inc(ones_made, 1)

    def pool_before(pool, v):
        if v == 8:
            pool_rstd(pool, 0)
        if v == 14:
            pool_rstd(pool, 1)
        if v == 16:
            pool_piece2(pool, 0)
        if v == 17:
            pool_bias(pool, 0)
            pool_bias(pool, 1)

    def sp_before(sp):
        sp.wait_ge(slot0_zeroed, 8)
        zero_rows = kq_dram[:, 3, 0].rearrange("b (d h) t -> b d (h t)", d=DH)[:, 0:KM - KP]
        sp.dma_start(zero_rows.rearrange("b d n -> d b n"), qa[0][0:(KM - KP)].rearrange("p h t -> p (h t)").unsqueeze(1).broadcast_to([KM - KP, NB, NH * S])).then_inc(zeros_out, 16)
        sp.wait_ge(zeros_out, 16)
        sp.wait_ge(ones_made, 1)
        sp_step(sp, -1, 3)

    def run(next_stage):
        nonlocal after, pt, nm, nmr, mp, mT, oT, rsum, otok, osp, oTs
        after = next_stage
        with ExitStack() as late:
            def sb(n, shape, dt=F32):
                return late.enter_context(nc.sbuf_tensor(f"attn_{n}", shape, dt))

            for i in range(1, 4):
                qa.append(sb(f"qa{i}", [P, NH, S], BF16)[:])
                ka.append(sb(f"ka{i}", [P, NH, S], BF16)[:])
                va.append(sb(f"va{i}", [P, 2, NH, 32]))
            pt = sb("pt", [P, 2, NJ, 2 * S])
            nm = sb("nm", [P, 2, NH])
            nmr = sb("nmr", [P, 2, NH])
            mp = sb("mp", [P, 2, 8, NH], BF16)
            mT = sb("mT", [3 * NH, S], BF16)
            oT = sb("oT", [P, 2 * S])
            rsum = sb("rsum", [P, 2, 2, NJ])
            otok = sb("otok", [P, 2, HALF])
            osp = sb("osp", [P, 2, 2, HALF])
            oTs = sb("oTs", [P, S], F32R)
            block = late.enter_context(nc.Block())

            @block.tensor
            def _(pe):
                run_steps(pe, pe_step)

            @block.scalar
            def _(act):
                run_steps(act, act_step)

            @block.gpsimd
            def _(pool):
                pool_slot_init(pool, 1)
                run_steps(pool, pool_step)

            @block.vector
            def _(dve):
                dve.memset(mp[:], 0.0).then_inc(mp_zero, 1)
                run_steps(dve, dve_step)

            @block.sync
            def _(sp):
                for s in range(NB + 3):
                    sp_step(sp, s, s % 4)
                after["sp_head"](sp)

    return dict(pe_before=pe_before, act_before=act_before, dve_before=dve_before,
                           pool_before=pool_before, pool_slot0=pool_slot0, sp_before=sp_before, run=run)


def kernel(L0_attn_x, L0_attn_Wq, L0_attn_Wk, L0_attn_Wv, L0_attn_Wo, L0_attn_bo, L0_ffn_gate_w,
           L0_ffn_gate_b, L0_ffn_w0, L0_ffn_b0, L0_ffn_w1, L0_ffn_b1, L0_ffn_w2, L0_ffn_b2):
    import numpy as np
    import concourse.bacc as bacc
    from concourse import mybir as mb
    from concourse.bass_utils import run_bass_kernel_spmd

    def np32(a):
        return np.asarray(a)

    def head_minor(w):
        return np32(w).reshape(NH, DH, HALF).transpose(1, 0, 2).reshape(HALF, HALF)

    arrays = {
        "x": np32(L0_attn_x),
        "gate_wT": np32(L0_ffn_gate_w).T,
        "gate_b": np32(L0_ffn_gate_b).reshape(E),
        "w0T": np32(L0_ffn_w0).transpose(2, 0, 1).reshape(P, E * HID),
        "b0T": np32(L0_ffn_b0).reshape(UNITS, P).T,
        "w1T": np32(L0_ffn_w1).transpose(2, 0, 1).reshape(P, E * HID),
        "b1T": np32(L0_ffn_b1).reshape(UNITS, P).T,
        "w2T": np32(L0_ffn_w2).reshape(E, P, CH, P).transpose(3, 0, 2, 1).reshape(P, E * HID),
        "b2": np32(L0_ffn_b2),
        "wqT": head_minor(L0_attn_Wq).T,
        "wkT": head_minor(L0_attn_Wk).T,
        "wvT": np32(L0_attn_Wv).T,
        "woT": np32(L0_attn_Wo).T,
        "bo": np32(L0_attn_bo),
    }
    arrays = {k: np.ascontiguousarray(v) for k, v in arrays.items()}
    nc = bacc.Bacc("TRN2", target_bir_lowering=False, num_devices=1)
    aps = {k: nc.dram_tensor(k, v.shape, F32, kind="ExternalInput").ap() for k, v in arrays.items()}
    out = nc.dram_tensor("out", (NB, S, P), F32, kind="ExternalOutput").ap()
    macaron(nc, **aps, out=out)
    r = run_bass_kernel_spmd(nc, [arrays], core_ids=[0])
    return r.results[0]["out"]
```
